# Optimizing a Trainium2 kernel written in Bass

```python
import numpy as np
import jax
import jax.numpy as jnp

def _softmax(x, axis=-1):
    return jax.nn.softmax(x, axis=axis)

def _gelu(x):
    return jax.nn.gelu(x, approximate=True)

def _silu(x):
    return jax.nn.silu(x)

def _sigmoid(x):
    return jax.nn.sigmoid(x)

def _layernorm(x, axis=-1, eps=1e-05):
    m = jnp.mean(x, axis=axis, keepdims=True)
    v = jnp.var(x, axis=axis, keepdims=True)
    return (x - m) / jnp.sqrt(v + eps)

def _scatter_add(tgt, idx, src, axis=0):
    return tgt.at[idx].add(src)

def _segment_sum(src, seg, n):
    return jax.ops.segment_sum(src, seg, n)
kernel_name = 'mk_gnn_resnorm_d2_gnn_r32_f36421'

def setup_inputs(seed: int=0):
    np.random.seed(seed)
    _w = jnp.asarray

    def _rec_inputs():
        import jax
        import jax.numpy as jnp
        _gk = jax.random.key(seed)
        x = 0.0002542 + 0.9999 * jax.random.normal(jax.random.fold_in(_gk, 1), (6250, 64), jnp.float32)
        src = jax.random.randint(jax.random.fold_in(_gk, 2), (100000,), 0, 6250, jnp.int32)
        dst = jax.random.randint(jax.random.fold_in(_gk, 3), (100000,), 0, 6250, jnp.int32)
        _o = jnp.argsort(dst, stable=True)
        src = src[_o]
        dst = dst[_o]
        edge_attr_32 = 0.000189758 + 1.00013 * jax.random.normal(jax.random.fold_in(_gk, 11), (100000, 32), jnp.float32)
        edge_type_2 = jax.random.randint(jax.random.fold_in(_gk, 13), (100000,), 0, 2, jnp.int32)
        return (x, src, dst, edge_attr_32, edge_type_2)
    x, src, dst, edge_attr_32, edge_type_2 = _rec_inputs()

    def _L0_gnn_setup():
        import jax, jax.numpy as jnp
        import numpy as np
        N_ENTITIES = 6250
        N_RELATIONS = 2
        EMBED_DIM = 64
        N_EDGES = 62500
        key = jax.random.key(seed)
        k1, k2, k3, k4, k5, k6, k7, k8 = jax.random.split(key, 8)
        edge_index = jax.random.randint(k1, (2, N_EDGES), 0, N_ENTITIES, dtype=jnp.int32)
        edge_type = jax.random.randint(k2, (N_EDGES,), 0, N_RELATIONS, dtype=jnp.int32)
        entity_emb = jax.random.normal(k3, (N_ENTITIES, EMBED_DIM), dtype=jnp.float32)
        relation_emb = jax.random.normal(k4, (N_RELATIONS, EMBED_DIM), dtype=jnp.float32)
        att_w = jax.random.normal(k5, (2 * EMBED_DIM, 1), dtype=jnp.float32) * 0.08
        att_b = jax.random.normal(k6, (1,), dtype=jnp.float32) * 0.08
        W_w = jax.random.normal(k7, (EMBED_DIM, EMBED_DIM), dtype=jnp.float32) * 0.12
        W_b = jax.random.normal(k8, (EMBED_DIM,), dtype=jnp.float32) * 0.12
        return {'edge_index': edge_index, 'edge_type': edge_type, 'entity_emb': entity_emb, 'relation_emb': relation_emb, 'att_w': att_w, 'att_b': att_b, 'W_w': W_w, 'W_b': W_b}
    _L0_gnn_all = _L0_gnn_setup()
    _L0_gnn_in = {k: v for k, v in _L0_gnn_all.items() if k in ('relation_emb', 'att_w', 'att_b', 'W_w', 'W_b')}
    del _L0_gnn_all

    def _L1_gnn_setup():
        import jax, jax.numpy as jnp
        import numpy as np
        N_NODES = 3125
        N_EDGES = 50000
        HID = 64
        EDIM = 32

        def _linear_params(key, fan_in, fan_out):
            kw, kb = jax.random.split(key)
            bound = 1.0 / np.sqrt(fan_in)
            w = jax.random.uniform(kw, (fan_in, fan_out), jnp.float32, -bound, bound)
            b = jax.random.uniform(kb, (fan_out,), jnp.float32, -bound, bound)
            return (w, b)
        key = jax.random.key(seed)
        ks = jax.random.split(key, 7)
        x = jax.random.normal(ks[0], (N_NODES, HID), jnp.float32)
        edge_index = jax.random.randint(ks[1], (2, N_EDGES), 0, N_NODES, jnp.int64)
        edge_attr = jax.random.normal(ks[2], (N_EDGES, EDIM), jnp.float32)
        ew1, eb1 = _linear_params(ks[3], 2 * HID + EDIM, HID)
        ew2, eb2 = _linear_params(ks[4], HID, HID)
        nw1, nb1 = _linear_params(ks[5], 2 * HID, HID)
        nw2, nb2 = _linear_params(ks[6], HID, HID)
        return {'x': x, 'edge_index': edge_index, 'edge_attr': edge_attr, 'ew1': ew1, 'eb1': eb1, 'ew2': ew2, 'eb2': eb2, 'nw1': nw1, 'nb1': nb1, 'nw2': nw2, 'nb2': nb2}
    _L1_gnn_all = _L1_gnn_setup()
    _L1_gnn_in = {k: v for k, v in _L1_gnn_all.items() if k in ('ew1', 'eb1', 'ew2', 'eb2', 'nw1', 'nb1', 'nw2', 'nb2')}
    del _L1_gnn_all
    return {'x': x, 'src': src, 'dst': dst, 'edge_attr_32': edge_attr_32, 'edge_type_2': edge_type_2, 'L0_gnn_relation_emb': _L0_gnn_in['relation_emb'], 'L0_gnn_att_w': _L0_gnn_in['att_w'], 'L0_gnn_att_b': _L0_gnn_in['att_b'], 'L0_gnn_W_w': _L0_gnn_in['W_w'], 'L0_gnn_W_b': _L0_gnn_in['W_b'], 'L1_gnn_ew1': _L1_gnn_in['ew1'], 'L1_gnn_eb1': _L1_gnn_in['eb1'], 'L1_gnn_ew2': _L1_gnn_in['ew2'], 'L1_gnn_eb2': _L1_gnn_in['eb2'], 'L1_gnn_nw1': _L1_gnn_in['nw1'], 'L1_gnn_nb1': _L1_gnn_in['nb1'], 'L1_gnn_nw2': _L1_gnn_in['nw2'], 'L1_gnn_nb2': _L1_gnn_in['nb2']}

def reference(x, src, dst, edge_attr_32, edge_type_2, L0_gnn_relation_emb, L0_gnn_att_w, L0_gnn_att_b, L0_gnn_W_w, L0_gnn_W_b, L1_gnn_ew1, L1_gnn_eb1, L1_gnn_ew2, L1_gnn_eb2, L1_gnn_nw1, L1_gnn_nb1, L1_gnn_nw2, L1_gnn_nb2):
    import jax
    import jax.numpy as jnp

    def _L0_gnn_ref(edge_index, edge_type, entity_emb, relation_emb, att_w, att_b, W_w, W_b):
        import jax, jax.numpy as jnp
        import numpy as np
        N_ENTITIES = 6250
        N_RELATIONS = 2
        EMBED_DIM = 64
        N_EDGES = 62500
        head = entity_emb[edge_index[0]]
        tail = entity_emb[edge_index[1]]
        rel = relation_emb[edge_type]
        head_rel = jnp.concatenate([head, rel], axis=-1)
        att_scores = jax.nn.sigmoid(head_rel @ att_w + att_b)
        neighbor_emb = att_scores * tail
        aggr_emb = jax.ops.segment_sum(neighbor_emb, edge_index[0], num_segments=N_ENTITIES)
        return jnp.tanh(aggr_emb @ W_w.T + W_b)

    def _L1_gnn_ref(x, edge_index, edge_attr, ew1, eb1, ew2, eb2, nw1, nb1, nw2, nb2):
        import jax, jax.numpy as jnp
        import numpy as np
        N_NODES = 3125
        N_EDGES = 50000
        HID = 64
        EDIM = 32

        def _linear_params(key, fan_in, fan_out):
            kw, kb = jax.random.split(key)
            bound = 1.0 / np.sqrt(fan_in)
            w = jax.random.uniform(kw, (fan_in, fan_out), jnp.float32, -bound, bound)
            b = jax.random.uniform(kb, (fan_out,), jnp.float32, -bound, bound)
            return (w, b)
        row, col = (edge_index[0], edge_index[1])
        edge_features = jnp.concatenate([x[row], x[col], edge_attr], axis=-1)
        h = jax.nn.relu(edge_features @ ew1 + eb1)
        messages = h @ ew2 + eb2
        aggregated = jax.ops.segment_sum(messages, row, num_segments=x.shape[0])
        out = jnp.concatenate([x, aggregated], axis=-1)
        out = jax.nn.relu(out @ nw1 + nb1)
        out = out @ nw2 + nb2
        return out
    edge_index = jnp.stack([src, dst])
    x = _layernorm(x + _L0_gnn_ref(edge_index, edge_type_2, x, L0_gnn_relation_emb, L0_gnn_att_w, L0_gnn_att_b, L0_gnn_W_w, L0_gnn_W_b), axis=-1)
    x = _layernorm(x + _L1_gnn_ref(x, edge_index, edge_attr_32, L1_gnn_ew1, L1_gnn_eb1, L1_gnn_ew2, L1_gnn_eb2, L1_gnn_nw1, L1_gnn_nb1, L1_gnn_nw2, L1_gnn_nb2), axis=-1)
    return x

_drawn_inputs = setup_inputs


def setup_inputs(seed=0):
    import zlib

    import numpy as np

    out = dict(_drawn_inputs(seed))
    spreads = {}
    factors = {'L1_gnn_nb1': 2.764}
    for name, (base, spread) in spreads.items():
        noise = np.random.default_rng([zlib.crc32(name.encode()), seed]).standard_normal(out[name].shape)
        drawn = base * np.exp(spread * noise) if base else spread * noise
        out[name] = jnp.asarray(drawn.astype(out[name].dtype))
    for name, factor in factors.items():
        out[name] = (out[name] * factor).astype(out[name].dtype)
    return out
```

```python
import concourse.bass as bass
from concourse import mybir
from contextlib import ExitStack

f32 = mybir.dt.float32
i32 = mybir.dt.int32
bf16 = mybir.dt.bfloat16
ALU = mybir.AluOpType
ACT = mybir.ActivationFunctionType
AX = mybir.AxisListType

N = 6250
E = 100000
D = 64
A = 32
P = 128
HI = -(-N // P)
TG = 16
GE = TG * P
EG = -(-E // GE)
EJ = EG * TG
TAIL = (E - (EG - 1) * GE) // TG
WIN = 2 * P
NB = HI + 1
B2 = 3 * NB // 4
ST = 832
SG = ST // TG
SS = ST + TG
FULL = E // P
R = D + A + 4
KEY, DST, TYP0, TYP1 = range(D + A, R)
TT = 7
C7 = 7
NC = HI // C7
W = D + 1
SLOTS = TG
L1B = 7
RANK_STEPS = 8
SPLIT_STEPS = 4
EPS = 1e-05
assert (EG - 1) * GE + TAIL * TG == E and HI == C7 * NC and TT * P >= ST
assert (E + (P - 1) * HI + HI) // P <= ST and EG % 2 == 1 and SG % 2 == 0
assert HI * P == 8 * EJ and FULL * P <= E and ST - FULL >= 0


def bass_gnn_two_layers(nc, x, src, dst, attr, etype, rel, att_w, att_b, WT, W_b,
                        ew1, eb1, ew2, eb2, nw1, nb1, nw2, nb2, out):
    sorted_rec = nc.dram_tensor("sorted_rec", (P * SS, R), f32, kind="Internal").ap()
    q_table = nc.dram_tensor("q_table", (HI * P, D), f32, kind="Internal").ap()
    tile_dram = nc.dram_tensor("tile_dram", (2, TT * P), i32, kind="Internal").ap()
    by_tile = sorted_rec.rearrange("(p t) r -> p t r", p=P)
    by_lane = sorted_rec.rearrange("(p t) r -> p (t r)", p=P)

    ctx = ExitStack()
    with ctx:
        def sb(name, shape, dt=f32):
            return ctx.enter_context(nc.sbuf_tensor(name, shape, dt))

        def sem(name):
            return ctx.enter_context(nc.semaphore(name))

        def sems(name, n):
            return [sem(f"{name}{k}") for k in range(n)]

        def merged(ap):
            return ap.rearrange("p a b -> p (a b)")

        early = sb("early", [P, 8 * EJ])
        src_i, dst_i, typ_i = (early[:, n * EJ:(n + 1) * EJ].bitcast(i32).rearrange("p (g k) -> p g k", k=TG) for n in range(3))
        lo_i = early[:, 3 * EJ:4 * EJ].bitcast(i32)
        meta = early[:, 4 * EJ:8 * EJ].rearrange("p (j r) -> p j r", r=4)
        hi_f = sb("hi_f", [P, EJ])
        attr_in = [sb(f"attr_in{s}", [P, TG, A]) for s in range(2)]
        rec = [sb(f"rec{s}", [P, TG, R]) for s in range(2)]
        place = [sb(f"place{s}", [P, TG], i32) for s in range(2)]
        xwin = [sb(f"xwin{s}", [P, 2, D]) for s in range(2)]
        xpart = [sb(f"xpart{s}", [P, 3, 2, D], bf16) for s in range(2)]
        xrest = sb("xrest", [P, 2, D])
        win_base = sb("win_base", [P, EG])
        in_win = sb("in_win", [P, EJ], bf16)
        win_i = sb("win_i", [P, EG], i32)
        far = sb("far", [P, 1])
        outside = sb("outside", [P, 1])
        slow_i = sb("slow_i", [P, 1], i32)
        count = sb("count", [P, NB])
        signs = sb("signs", [P, NB])
        half_b = sb("half_b", [P, NB])
        iota_b = sb("iota_b", [P, NB])
        iota_w = sb("iota_w", [P, 2])
        lower = sb("lower", [P, P])
        first_row = sb("first_row", [P, P])
        ones = sb("ones", [P, P])
        before = sb("before", [P, NB])
        total = sb("total", [P, NB])
        tiles_i = sb("tiles_i", [P, NB], i32)
        tiles_j = sb("tiles_j", [P, NB], i32)
        tiles_f = sb("tiles_f", [P, NB])
        tile_end = sb("tile_end", [P, NB])
        ends_i = sb("ends_i", [P, NB], i32)
        reset = sb("reset", [P, NB, TG + 1])
        marks = sb("marks", [P, NB, TG + 1])
        ranks = sb("ranks", [P, NB, TG + 1])
        picked = sb("picked", [P, NB, TG])
        off = picked[:, 0:EG, :]
        base = sb("base", [P, NB])
        pos_f = sb("pos_f", [P, TG])
        pos_i = sb("pos_i", [P, TG], i32)
        pos_j = sb("pos_j", [P, TG], i32)
        pos_k = sb("pos_k", [P, TG], i32)
        t_i = sb("t_i", [P, 2, TT], i32)
        t_f = sb("t_f", [P, 2, TT])
        t_cmp = merged(ranks[:, :, :])[:, 0:2 * TT * (HI - 1)].rearrange("p (t b) -> p t b", b=HI - 1)
        t_hi = sb("t_hi", [P, 2, TT])
        t_slot = sb("t_slot", [P, TT])
        t_out = sb("t_out", [P, 2, TT], i32)
        tile_hi = sb("tile_hi", [1, TT * P], i32)
        tile_slot = sb("tile_slot", [1, TT * P], i32)
        gidx = [sb(f"gidx{s}", [P, TG], i32) for s in range(2)]
        iota_lo = sb("iota_lo", [P, P])
        ident = sb("ident", [P, P])
        ident_h = sb("ident_h", [P, P], bf16)
        hot_all = sb("hot_all", [P, 2, TG * P])
        hot = [hot_all[:, s, :].rearrange("p (t e) -> p t e", e=P) for s in range(2)]
        win_hot = [hot_all[:, s, :].bitcast(bf16).rearrange("p (w e) -> p w e", w=2) for s in range(2)]
        both = [sb(f"both{s}", [P, TG, 2 * D]) for s in range(2)]
        zeros = sb("zeros", [P, 512], bf16)
        zero_rec = sb("zero_rec", [P, 1, R])
        acc0 = sb("acc0", [P, HI + SLOTS, 2 * D])
        junk_dve, junk_act, hi_h = (merged(acc0[:, 8 * n:8 * n + 4, :]).bitcast(bf16)[:, 0:EJ] for n in range(3))
        xs = sb("xs", [P, HI, D])
        att = sb("att", [P, 2, HI])
        xw = sb("xw", [P, HI])
        wide = sb("wide", [P, 2, D])
        relw = sb("relw", [P, 2])
        attw_b = sb("attw_b", [P, 2, D])
        attb_b = sb("attb_b", [P, 1])
        rel_b = sb("rel_b", [P, 2, D])
        W65 = sb("W65", [W, D])
        Eab = sb("Eab", [W, 2 * D])
        ec_blk = sb("ec_blk", [P, 4, D])
        ew2_65 = sb("ew2_65", [W, D])
        na65 = sb("na65", [W, D])
        nb64 = sb("nb64", [D, D])
        nw2_65 = sb("nw2_65", [W, D])
        eps = sb("eps", [P, 1])
        x1 = sb("x1", [P, HI, W])
        x1T = early[0:W, :]
        ptab = sb("ptab", [P, HI, D])
        acc1 = sb("acc1", [P, HI + 3 * L1B, W])
        aggr = [sb(f"aggr{s}", [P, C7, W]) for s in range(2)]
        part = [hot_all[:, 0, r * C7 * D:(r + 1) * C7 * D].rearrange("p (h d) -> p h d", d=D) for r in range(2)]
        tmp, th = (merged(both[s][:, 0:4, :])[:, 0:C7 * D].rearrange("p (h d) -> p h d", d=D) for s in range(2))
        mean = sb("mean", [P, C7])
        var = sb("var", [P, HI])
        dev = sb("dev", [P, HI])
        rstd = sb("rstd", [P, HI])
        srec1 = [merged(rec[s][:, :, :])[:, 0:TG * (A + 4)].rearrange("p (t r) -> p t r", r=A + 4) for s in range(2)]
        qrow = [merged(both[s][:, 0:8, :]).rearrange("p (t d) -> p t d", d=D) for s in range(2)]
        pre = [merged(both[s][:, 8:16, :]).rearrange("p (t d) -> p t d", d=D) for s in range(2)]
        attrT = [acc0[:, 8 * s:8 * s + 4, :] for s in range(2)]
        hrow = [merged(acc0[:, 16 + 10 * s:16 + 10 * s + 9, :])[:, 0:TG * W].rearrange("p (t w) -> p t w", w=W) for s in range(2)]
        hotT = acc0[:, 36:52, :]
        q_out = merged(acc0[:, 40:65, :])[:, 0:HI * D].rearrange("p (h d) -> p h d", d=D)
        agT = hot_all[0:D, 0, 0:C7 * P]
        hidT = hot_all[0:W, 0, P * 8:P * 8 + C7 * P]
        hT = hot_all[0:W, 1, 0:C7 * P]
        nT = hT

        psum = ctx.enter_context(nc.psum_tensor("psum", [P, 8, 512], f32))
        banks = psum[:, :, :].rearrange("p b n -> p (b n)")
        win_T = [banks[:, 1024 * s:1024 * (s + 1)].bitcast(bf16) for s in range(2)]
        CW = C7 * P
        pair = lambda b: banks[:, 512 * b:512 * b + CW]

        src_loaded = sem("src_loaded")
        loaded = sem("loaded")
        node_in = sem("node_in")
        memset_done = sem("memset_done")
        tail_zeroed = sem("tail_zeroed")
        zeroed = sem("zeroed")
        prep = sem("prep")
        act_counted = sem("act_counted")
        sums_ready = sem("sums_ready")
        table_out = sem("table_out")
        table_in = sem("table_in")
        attr_loaded = sems("attr_loaded", 2)
        xwin_in = sems("xwin_in", 2)
        split_step = sem("split_step")
        dstT_done = sem("dstT_done")
        win_hot_ready = sem("win_hot_ready")
        x_rows_done = sem("x_rows_done")
        xidx_ready = sem("xidx_ready")
        x_gathered = sems("x_gathered", 2)
        rec_ready = sem("rec_ready")
        place_ready = sem("place_ready")
        rank_step = sem("rank_step")
        scattered = sems("scattered", 2)
        att_step = sem("att_step")
        att_ready = sem("att_ready")
        srec0_in = sems("srec0_in", 2)
        hot0_ready = sem("hot0_ready")
        both0_ready = sem("both0_ready")
        sums0 = sem("sums0")
        added0 = sem("added0")
        agg_step = sem("agg_step")
        n_agg = sem("n_agg")
        n_T1 = sem("n_T1")
        n_T1c = sem("n_T1c")
        n_lin = sem("n_lin")
        n_th = sem("n_th")
        n_step = sem("n_step")
        n_dev = sem("n_dev")
        n_x1 = sem("n_x1")
        n_T2 = sem("n_T2")
        n_T2c = sem("n_T2c")
        n_pq = sem("n_pq")
        n_p = sem("n_p")
        n_q = sem("n_q")
        q_stored = sem("q_stored")
        srec1_in = sems("srec1_in", 2)
        idx1_ready = sem("idx1_ready")
        rows1_in = sems("rows1_in", 2)
        hot1_ready = sem("hot1_ready")
        attr_packed = sem("attr_packed")
        attrT_done = sem("attrT_done")
        attrT_copied = sem("attrT_copied")
        hotT_done = sem("hotT_done")
        hotT_copied = sem("hotT_copied")
        pre_done = sem("pre_done")
        pre_added = sem("pre_added")
        h_ready = sem("h_ready")
        sums1 = sem("sums1")
        added1 = sem("added1")
        ones_set = sem("ones_set")
        f_T = sem("f_T")
        f_Tc = sem("f_Tc")
        f_ag = sem("f_ag")
        f_agc = sem("f_agc")
        f_hid = sem("f_hid")
        f_hidc = sem("f_hidc")
        f_out = sem("f_out")
        f_step = sem("f_step")
        f_dev = sem("f_dev")
        f_ready = sem("f_ready")
        stored = sem("stored")

        at = {}
        block = ctx.enter_context(nc.Block())

        def zero_last_tiles(eng, start, stop):
            eng.wait_ge(prep, at["ends"])
            eng.wait_ge(tail_zeroed, 16)
            ends = [eng.alloc_register(f"end{k}") for k in range(C7)]
            with eng.Fori(start, stop) as i:
                eng.load(ends, ends_i[0:1, bass.ts(i, C7)])
                for k in range(C7):
                    end = eng.snap(ends[k], min_val=0, max_val=ST - 1)
                    eng.dma_start(by_tile[:, bass.ds(end, 1), :], zero_rec[:, :, :]).then_inc(zeroed, 16)

        @block.vector
        def _(dve):
            def chain(semaphore, start=0):
                n = [0]

                def step(ins):
                    n[0] += 1
                    ins.then_inc(semaphore, 1)
                    dve.wait_ge(semaphore, start + n[0])
                return step, n

            step, n = chain(prep)
            dve.wait_ge(memset_done, 6)
            step(dve.tensor_scalar(half_b[:, :], iota_b[:, :], -1.0, 0.5, ALU.mult, ALU.add))
            dve.wait_ge(src_loaded, 32)
            src2, dst2, typ2 = merged(src_i), merged(dst_i), merged(typ_i)
            step(dve.tensor_scalar(lo_i, src2, 7, None, ALU.logical_shift_right))
            step(dve.tensor_copy(hi_f[:, :], lo_i))
            at["hi"] = n[0]
            step(dve.tensor_copy(hi_h[:, :], hi_f[:, :]))
            for b in range(B2):
                step(dve.tensor_scalar(junk_dve[:, :], hi_h[:, :], float(b), None, ALU.is_equal, ALU.add,
                                       accum_out=count[:, b:b + 1]))
            dve.wait_ge(act_counted, NB - B2)
            step(dve.tensor_tensor(count[:, B2:NB - 1], signs[:, B2:NB - 1], signs[:, B2 + 1:NB], ALU.subtract))
            step(dve.tensor_scalar(count[:, B2:NB - 1], count[:, B2:NB - 1], 0.5, None, ALU.mult))
            step(dve.tensor_scalar(count[:, NB - 1:NB], signs[:, NB - 1:NB], 0.5, EJ / 2, ALU.mult, ALU.add))
            at["count"] = n[0]
            dve.wait_ge(loaded, 64)
            step(dve.tensor_scalar(lo_i, src2, P - 1, None, ALU.bitwise_and))
            step(dve.tensor_scalar(meta[:, :, 0], lo_i, 1, None, ALU.add))
            step(dve.tensor_copy(meta[:, :, 1], dst2))
            step(dve.tensor_copy(meta[:, :, 3], typ2))
            step(dve.tensor_scalar(meta[:, :, 2], meta[:, :, 3], -1.0, 1.0, ALU.mult, ALU.add))
            at["meta"] = n[0]
            dve.wait_ge(sums_ready, 1)
            step(dve.tensor_copy(before[:, :], psum[:, 0, 0:NB]))
            step(dve.tensor_copy(total[:, :], psum[:, 0, 64:64 + NB]))
            step(dve.tensor_scalar(tiles_i[:, :], total[:, :], float(P - 1), float(P), ALU.add, ALU.max))
            step(dve.tensor_scalar(tiles_j[:, :], tiles_i[:, :], 7, None, ALU.logical_shift_right))
            step(dve.tensor_copy(tiles_f[:, :], tiles_j[:, :]))
            step(dve.tensor_tensor_scan(tile_end[:, :], tiles_f[:, :], ones[:, 0:NB], 0.0, ALU.add, ALU.mult))
            step(dve.tensor_scalar(ends_i[:, :], tile_end[:, :], -1.0, None, ALU.add))
            at["ends"] = n[0]
            dve.wait_ge(sums_ready, 2)
            step(dve.tensor_scalar(win_base[:, :], psum[:, 1, 0:EG], float(N - WIN), None, ALU.min))
            step(dve.tensor_copy(win_i[:, :], win_base[:, :]))
            step(dve.tensor_tensor(off[:, :, :], meta[:, :, 1].rearrange("p (g k) -> p g k", k=TG),
                                   win_base[:, :].unsqueeze(2).to_broadcast([P, EG, TG]), ALU.subtract))
            step(dve.tensor_copy(in_win[:, :], merged(off[:, :, :])))
            step(dve.tensor_scalar(off[:, :, :], off[:, :, :], -(WIN - 1) / 2, None, ALU.add))
            step(dve.tensor_tensor(off[:, :, :], off[:, :, :], off[:, :, :], ALU.mult))
            step(dve.tensor_reduce(far[:, :], merged(off[:, :, :]), AX.X, ALU.max))
            step(dve.tensor_scalar(outside[:, :], far[:, :], float(P * P), None, ALU.is_ge))
            at["outside"] = n[0]
            step(dve.tensor_tensor(base[:, :], tile_end[:, :], tiles_f[:, :], ALU.subtract))
            step(dve.memset(base[:, HI:NB], float(ST)))
            step(dve.tensor_scalar(base[:, :], base[:, :], float(P), None, ALU.mult))
            step(dve.tensor_tensor(marks[:, :, 0], base[:, :], before[:, :], ALU.add))
            dve.wait_ge(sums_ready, 3)
            step(dve.tensor_copy(slow_i[:, :], psum[:, 2, 0:1]))
            at["slow"] = n[0]

            def rank(g, s, n_slot):
                m = [0]

                def rstep(ins):
                    m[0] += 1
                    ins.then_inc(rank_step, 1)
                    dve.wait_ge(rank_step, g * RANK_STEPS + m[0])
                rstep(dve.tensor_tensor(marks[:, :, 1:TG + 1], hi_f[:, bass.ts(g, TG)].unsqueeze(1).to_broadcast([P, NB, TG]),
                                        iota_b[:, :].unsqueeze(2).to_broadcast([P, NB, TG]), ALU.is_equal))
                rstep(dve.tensor_tensor_scan(merged(ranks[:, :, :]), merged(reset[:, :, :]), merged(marks[:, :, :]),
                                             0.0, ALU.mult, ALU.add))
                rstep(dve.tensor_tensor(picked[:, :, :], marks[:, :, 1:TG + 1], ranks[:, :, 1:TG + 1], ALU.mult))
                rstep(dve.tensor_copy(marks[:, :, 0], ranks[:, :, TG]))
                rstep(dve.tensor_reduce(pos_f[:, :], picked[:, :, :].rearrange("p b k -> p k b"), AX.X, ALU.add))
                rstep(dve.tensor_scalar(pos_i[:, :], pos_f[:, :], -1.0, None, ALU.add))
                rstep(dve.tensor_scalar(pos_j[:, :], pos_i[:, :], P - 1, None, ALU.bitwise_and))
                rstep(dve.tensor_scalar(pos_k[:, :], pos_i[:, :], 7, None, ALU.logical_shift_right))
                if n_slot is not None:
                    dve.wait_ge(scattered[s], 16 * TG * n_slot)
                dve.scalar_tensor_tensor(place[s][:, :], pos_j[:, :], float(SS), pos_k[:, :], ALU.mult, ALU.add).then_inc(place_ready, 1)
                assert m[0] == RANK_STEPS

            def window_matrices(g, s, n_slot):
                dve.wait_ge(dstT_done, g + 1)
                if n_slot is not None:
                    dve.wait_ge(x_rows_done, g - 1)
                for w in range(2):
                    ins = dve.tensor_scalar(win_hot[s][:, w, :], win_T[s], iota_w[:, w:w + 1], None, ALU.is_equal)
                ins.then_inc(win_hot_ready, 1)

            def split_window(g, s, n_slot):
                m = [0]

                def sstep(ins):
                    m[0] += 1
                    ins.then_inc(split_step, 1)
                    dve.wait_ge(split_step, g * SPLIT_STEPS + m[0])
                dve.wait_ge(xwin_in[s], 16 * (1 if n_slot is None else n_slot + 1))
                hi, mid, lo = (xpart[s][:, k, :, :] for k in range(3))
                sstep(dve.tensor_copy(hi, xwin[s][:, :, :]))
                sstep(dve.tensor_tensor(xrest[:, :, :], xwin[s][:, :, :], hi, ALU.subtract))
                sstep(dve.tensor_copy(mid, xrest[:, :, :]))
                sstep(dve.tensor_tensor(lo, xrest[:, :, :], mid, ALU.subtract))
                assert m[0] == SPLIT_STEPS

            def indices(g, s, n_slot):
                if n_slot is not None:
                    dve.wait_ge(x_gathered[s], 16 * TG * n_slot)
                dve.tensor_copy(gidx[s][:, :], meta[:, bass.ts(g, TG), 1]).then_inc(xidx_ready, 1)

            def places(fast):
                def group(g, s, n_slot):
                    if fast:
                        window_matrices(g, s, n_slot)
                        split_window(g, s, n_slot)
                    else:
                        indices(g, s, n_slot)
                    rank(g, s, n_slot)
                group(0, 0, None)
                group(1, 1, None)
                with dve.Fori(1, EG // 2) as i:
                    for s in range(2):
                        group(2 * i + s, s, i)
                group(EG - 1, 0, EG // 2)

            slow = dve.value_load(slow_i[0:1, 0:1], min_val=0, max_val=P)
            with dve.If(slow == 0):
                places(True)
            with dve.Else():
                places(False)

            step, n = chain(prep, n[0])
            before_table = at["slow"]
            dve.wait_ge(memset_done, MEMSETS)
            step(dve.tensor_scalar(t_i[:, 1, :], t_i[:, 0, :], 4, 4, ALU.logical_shift_right, ALU.logical_shift_left))
            step(dve.tensor_copy(t_f[:, :, :], t_i[:, :, :]))
            step(dve.tensor_tensor(t_cmp[:, :, :], merged(t_f[:, :, :]).unsqueeze(2).to_broadcast([P, 2 * TT, HI - 1]),
                                   tile_end[:, 0:HI - 1].unsqueeze(1).to_broadcast([P, 2 * TT, HI - 1]), ALU.is_ge))
            step(dve.tensor_reduce(merged(t_hi[:, :, :]), t_cmp[:, :, :], AX.X, ALU.add))
            step(dve.tensor_tensor(t_slot[:, :], t_hi[:, 0, :], t_hi[:, 1, :], ALU.subtract))
            step(dve.tensor_copy(t_out[:, 0, :], t_hi[:, 0, :]))
            step(dve.tensor_copy(t_out[:, 1, :], t_slot[:, :]))
            at["table"] = before_table + n[0]

            dve.wait_ge(node_in, 16 * 21)
            step, n = chain(att_step)
            big = acc0[:, 0:HI, 0:D]
            step(dve.tensor_tensor(big, xs[:, :, :], attw_b[:, 0, :].unsqueeze(1).to_broadcast([P, HI, D]), ALU.mult))
            step(dve.tensor_reduce(xw[:, :], big, AX.X, ALU.add))
            step(dve.tensor_tensor(wide[:, :, :], rel_b[:, :, :], attw_b[:, 1, :].unsqueeze(1).to_broadcast([P, 2, D]), ALU.mult))
            step(dve.tensor_reduce(relw[:, :], wide[:, :, :], AX.X, ALU.add))
            step(dve.tensor_scalar(relw[:, :], relw[:, :], attb_b[:, 0:1], None, ALU.add))
            at["att"] = n[0]

            dve.memset(acc0[:, :, :], 0.0).then_inc(added0, 1)
            for s in range(2):
                dve.memset(aggr[s][:, :, D:W], 1.0)
            dve.memset(x1[:, :, D:W], 1.0)
            dve.memset(acc1[:, :, :], 0.0).then_inc(added1, 1)
            iota_bc = iota_lo[:, :].unsqueeze(1).to_broadcast([P, TG, P])

            def hot_matrix(s, key):
                return dve.tensor_tensor(hot[s][:, :, :], iota_bc, key.unsqueeze(2).to_broadcast([P, TG, P]), ALU.is_equal)

            def edges0(g, s, n_slot, first):
                dve.wait_ge(srec0_in[s], 16 * n_slot)
                if not first:
                    dve.wait_ge(sums0, g - 1)
                hot_matrix(s, rec[s][:, :, KEY]).then_inc(hot0_ready, 1)

            def add0(g, s):
                h0 = dve.value_load(tile_hi[0:1, bass.ds(g * TG, 1)], min_val=0, max_val=HI - 1)
                dve.wait_ge(sums0, g + 1)
                dve.wait_ge(added0, g + 1)
                view = merged(acc0[:, :, :])[:, bass.ds(h0 * (2 * D), SLOTS * 2 * D)]
                dve.tensor_tensor(view, banks[:, 2048 * s:2048 * s + SLOTS * 2 * D], view, ALU.add).then_inc(added0, 1)

            dve.wait_ge(table_in, 32)
            for s in range(2):
                edges0(s, s, 1, True)
            with dve.Fori(1, SG // 2) as i:
                for s in range(2):
                    edges0(2 * i + s, s, i + 1, False)
                    add0(2 * i + s - 2, s)
            for s in range(2):
                add0(SG - 2 + s, s)

            def centre(rstep, rows, target, hs):
                rstep(dve.tensor_reduce(mean[:, :], rows, AX.X, ALU.add))
                rstep(dve.tensor_scalar(mean[:, :], mean[:, :], 1.0 / D, None, ALU.mult))
                rstep(dve.tensor_tensor(target, rows, mean[:, :].unsqueeze(2).to_broadcast([P, C7, D]), ALU.subtract))
                rstep(dve.tensor_tensor(tmp[:, :, :], target, target, ALU.mult))
                rstep(dve.tensor_reduce(var[:, hs], tmp[:, :, :], AX.X, ALU.add))

            step, n = chain(n_step)
            chunks = [slice(c * C7, (c + 1) * C7) for c in range(NC)]
            for c, hs in enumerate(chunks):
                dve.wait_ge(n_th, c + 1)
                step(dve.tensor_tensor(th[:, :, :], th[:, :, :], xs[:, hs, :], ALU.add))
                centre(step, th[:, :, :], x1[:, hs, 0:D], hs)
                at["th", c] = n[0] - 2
            at["var"] = n[0]
            dve.wait_ge(n_dev, 1)
            step(dve.reciprocal(rstd[:, :], dev[:, :]))
            for c in range(NC + 1):
                if c < NC:
                    hs = chunks[c]
                    dve.tensor_tensor(x1[:, hs, 0:D], x1[:, hs, 0:D], rstd[:, hs].unsqueeze(2).to_broadcast([P, C7, D]), ALU.mult).then_inc(n_x1, 1)
                if c >= 1:
                    dve.wait_ge(n_p, c)
                    dve.tensor_copy(q_out[:, chunks[c - 1], :], pair(4 + 2 * ((c - 1) % 2)).rearrange("p (h w) -> p h w", w=2 * D)[:, :, D:2 * D]).then_inc(n_q, 1)

            def edges1(g, s, n_slot, first):
                dve.wait_ge(srec1_in[s], 16 * n_slot)
                if not first:
                    dve.wait_ge(rows1_in[s], 16 * TG * (n_slot - 1))
                dve.tensor_copy(gidx[s][:, :], srec1[s][:, :, DST - D]).then_inc(idx1_ready, 1)
                if not first:
                    dve.wait_ge(sums1, g - 1)
                hot_matrix(s, srec1[s][:, :, KEY - D]).then_inc(hot1_ready, 1)

            def add_q(g, s, n_slot, first):
                dve.wait_ge(rows1_in[s], 16 * TG * n_slot)
                for q in range(4):
                    dve.wait_ge(pre_done, 4 * g + q + 1)
                    if not first:
                        dve.wait_ge(h_ready, 4 * g + q - 7)
                    dve.tensor_tensor(pre[s][:, 4 * q:4 * q + 4, :],
                                      psum[:, 6 + q % 2, 0:4 * D].rearrange("p (t d) -> p t d", d=D),
                                      qrow[s][:, 4 * q:4 * q + 4, :], ALU.add).then_inc(pre_added, 1)

            def add1(g):
                h0 = dve.value_load(tile_hi[0:1, bass.ds(g * TG, 1)], min_val=0, max_val=HI - 1)
                dve.wait_ge(sums1, g + 1)
                dve.wait_ge(added1, g + 1)
                view = merged(acc1[:, :, :])[:, bass.ds(h0 * W, 3 * L1B * W)].rearrange("p (b n) -> p b n", b=3)
                dve.tensor_tensor(view, psum[:, 0:3, 0:L1B * W], view, ALU.add).then_inc(added1, 1)

            for s in range(2):
                edges1(s, s, 1, True)
            for s in range(2):
                add_q(s, s, 1, True)
                add1(s)
                edges1(2 + s, s, 2, False)
            with dve.Fori(2, SG // 2) as i:
                for s in range(2):
                    add_q(2 * i + s - 2, s, i, False)
                    add1(2 * i + s - 2)
                    edges1(2 * i + s, s, i + 1, False)
            for s in range(2):
                add_q(SG - 2 + s, s, SG // 2, False)
                add1(SG - 2 + s)

            step, n = chain(f_step)
            for c, hs in enumerate(chunks):
                dve.wait_ge(f_out, c + 1)
                step(dve.tensor_tensor(th[:, :, :], psum[:, 6 + c % 2, 0:C7 * D].rearrange("p (h d) -> p h d", d=D), x1[:, hs, 0:D], ALU.add))
                at["out", c] = n[0]
                centre(step, th[:, :, :], xs[:, hs, :], hs)
            at["var1"] = n[0]
            dve.wait_ge(f_dev, 1)
            step(dve.reciprocal(rstd[:, :], dev[:, :]))
            for hs in chunks:
                dve.tensor_tensor(xs[:, hs, :], xs[:, hs, :], rstd[:, hs].unsqueeze(2).to_broadcast([P, C7, D]), ALU.mult).then_inc(f_ready, 1)

        @block.sync
        def _(sp):
            sp.wait_ge(memset_done, 3)
            for a, t, done in ((src, src_i, src_loaded), (dst, dst_i, loaded), (etype, typ_i, loaded)):
                full = a[0:(EG - 1) * GE].rearrange("(g p k) -> p g k", p=P, k=TG)
                sp.dma_start(t[:, 0:EG - 1, :], full).then_inc(done, 16)
                sp.dma_start(t[0:TAIL, EG - 1, :], a[(EG - 1) * GE:E].rearrange("(p k) -> p k", k=TG)).then_inc(done, 16)

            sp.wait_ge(memset_done, 15)
            last = (HI - 1) * P
            sp.dma_start(xs[:, 0:HI - 1, :], x[0:last, :].rearrange("(h p) d -> p h d", p=P)).then_inc(node_in, 16)
            sp.dma_start(xs[0:N - last, HI - 1, :], x[last:N, :]).then_inc(node_in, 16)
            sp.dma_start(attw_b[:, :, :], att_w.rearrange("(h d) o -> o h d", h=2).to_broadcast([P, 2, D])).then_inc(node_in, 16)
            sp.dma_start(attb_b[:, :], att_b.unsqueeze(0).to_broadcast([P, 1])).then_inc(node_in, 16)
            sp.dma_start(rel_b[:, :, :], rel.unsqueeze(0).to_broadcast([P, 2, D])).then_inc(node_in, 16)
            for w, b, t in ((WT, W_b, W65[:, :]), (ew1[0:D, :], eb1, Eab[:, 0:D]), (ew2, eb2, ew2_65[:, :]),
                            (nw1[0:D, :], nb1, na65[:, :]), (nw2, nb2, nw2_65[:, :])):
                sp.dma_start(t[0:D, :], w).then_inc(node_in, 16)
                sp.dma_start(t[D:W, :], b.unsqueeze(0)).then_inc(node_in, 16)
            sp.dma_start(Eab[0:D, D:2 * D], ew1[D:2 * D, :]).then_inc(node_in, 16)
            sp.dma_start(nb64[:, :], nw1[D:2 * D, :]).then_inc(node_in, 16)
            for q in range(4):
                sp.dma_start(ec_blk[A * q:A * (q + 1), q, :], ew1[2 * D:2 * D + A, :]).then_inc(node_in, 16)

            attr_v = attr.rearrange("e a -> (e a)")

            def load_attr(g, s):
                sp.dma_start(merged(attr_in[s][:, :, :]),
                             attr_v[bass.ts(g, GE * A)].rearrange("(p n) -> p n", p=P)).then_inc(attr_loaded[s], 16)

            def load_window(g, s):
                first = sp.value_load(win_i[0:1, bass.ds(g, 1)], min_val=0, max_val=N - WIN)
                sp.dma_start(xwin[s][:, :, :], x[bass.ds(first, WIN), :].rearrange("(w p) d -> p w d", p=P)).then_inc(xwin_in[s], 16)

            for s in range(2):
                load_attr(s, s)
            zero_last_tiles(sp, 0, SP_ZEROES)

            def loads(fast):
                if fast:
                    for s in range(2):
                        load_window(s, s)
                with sp.Fori(1, EG // 2) as i:
                    for s in range(2):
                        sp.wait_ge(rec_ready, 2 * i + s - 1)
                        load_attr(2 * i + s, s)
                        if fast:
                            sp.wait_ge(split_step, (2 * i + s - 1) * SPLIT_STEPS)
                            load_window(2 * i + s, s)
                sp.wait_ge(rec_ready, EG - 2)
                sp.dma_start(merged(attr_in[0][0:TAIL, :, :]),
                             attr_v[(EG - 1) * GE * A:E * A].rearrange("(p n) -> p n", p=TAIL)).then_inc(attr_loaded[0], 16)
                if fast:
                    sp.wait_ge(split_step, (EG - 2) * SPLIT_STEPS)
                    load_window(EG - 1, 0)

            sp.wait_ge(prep, at["slow"])
            slow = sp.value_load(slow_i[0:1, 0:1], min_val=0, max_val=P)
            with sp.If(slow == 0):
                loads(True)
            with sp.Else():
                loads(False)

            sp.wait_ge(prep, at["table"])
            for r in range(2):
                sp.dma_start(tile_dram[r:r + 1, :].rearrange("o (p k) -> (o p) k", k=TT), t_out[:, r, :]).then_inc(table_out, 16)
            sp.wait_ge(table_out, 32)
            for r, t in enumerate((tile_hi, tile_slot)):
                sp.dma_start(t[:, :], tile_dram[r:r + 1, :]).then_inc(table_in, 16)

            sp.wait_ge(scattered[0], 16 * TG * (EG // 2 + 1))
            sp.wait_ge(scattered[1], 16 * TG * (EG // 2))

            def load_sorted0(g, s):
                sp.dma_start(merged(rec[s][:, :, :]), by_lane[:, bass.ts(g, TG * R)]).then_inc(srec0_in[s], 16)

            def load_sorted1(g, s):
                sp.dma_start(srec1[s], by_tile[:, bass.ts(g, TG), D:R]).then_inc(srec1_in[s], 16)

            for s in range(2):
                load_sorted0(s, s)
            with sp.Fori(1, SG // 2) as i:
                for s in range(2):
                    sp.wait_ge(both0_ready, 2 * i + s - 1)
                    sp.wait_ge(hot0_ready, 2 * i + s - 1)
                    load_sorted0(2 * i + s, s)

            for s in range(2):
                sp.wait_ge(both0_ready, SG - 1 + s)
                sp.wait_ge(hot0_ready, SG - 1 + s)
                load_sorted1(s, s)

            for c in range(NC):
                sp.wait_ge(n_q, c + 1)
                sp.dma_start(q_table.rearrange("(h p) d -> p h d", p=P)[:, c * C7:(c + 1) * C7, :],
                             q_out[:, c * C7:(c + 1) * C7, :]).then_inc(q_stored, 16)

            with sp.Fori(1, SG // 2) as i:
                for s in range(2):
                    sp.wait_ge(hot1_ready, 2 * i + s - 1)
                    sp.wait_ge(attr_packed, 2 * i + s - 1)
                    load_sorted1(2 * i + s, s)

            for c in range(NC):
                sp.wait_ge(f_ready, c + 1)
                rows = min(C7 * P, N - c * C7 * P)
                full = rows // P
                o = out[c * C7 * P:c * C7 * P + full * P, :].rearrange("(h p) d -> p h d", p=P)
                sp.dma_start(o, xs[:, c * C7:c * C7 + full, :]).then_inc(stored, 16)
                if rows % P:
                    sp.dma_start(out[N - rows % P:N, :], xs[0:rows % P, HI - 1, :]).then_inc(stored, 16)
            sp.wait_ge(stored, 16 * (NC + 1))

        @block.gpsimd
        def _(pool):
            pool.memset(src_i[:, EG - 1, :], HI * P).then_inc(memset_done, 1)
            pool.memset(dst_i[:, EG - 1, :], N - 1).then_inc(memset_done, 1)
            pool.memset(typ_i[:, EG - 1, :], 0).then_inc(memset_done, 1)
            pool.memset(zero_rec[:, :, :], 0.0).then_inc(memset_done, 1)
            pool.iota(iota_b[:, :], [[1, NB]], base=0, channel_multiplier=0,
                      allow_small_or_imprecise_dtypes=True).then_inc(memset_done, 1)
            pool.memset(ones[:, :], 1.0).then_inc(memset_done, 1)
            pool.iota(iota_lo[:, :], [[1, P]], base=1, channel_multiplier=0,
                      allow_small_or_imprecise_dtypes=True).then_inc(memset_done, 1)
            pool.iota(iota_w[:, :], [[P, 2]], base=0, channel_multiplier=1,
                      allow_small_or_imprecise_dtypes=True).then_inc(memset_done, 1)
            pool.memset(reset[:, :, :], 1.0).then_inc(memset_done, 1)
            pool.memset(first_row[:, :], 0.0).then_inc(memset_done, 1)
            pool.memset(zeros[:, :], 0.0).then_inc(memset_done, 1)
            pool.memset(ec_blk[:, :, :], 0.0).then_inc(memset_done, 1)
            pool.memset(eps[:, :], EPS).then_inc(memset_done, 1)
            pool.memset(Eab[:, :], 0.0).then_inc(memset_done, 1)
            pool.memset(xs[:, HI - 1, :], 0.0).then_inc(memset_done, 1)
            pool.wait_ge(memset_done, 15)
            pool.memset(reset[:, :, 0:1], 0.0).then_inc(memset_done, 1)
            pool.memset(first_row[0:1, :], 1.0).then_inc(memset_done, 1)
            pool.affine_select(out=lower[:, :], in_=ones[:, :], compare_op=ALU.is_gt, fill=0.0, base=0,
                               pattern=[[1, P]], channel_multiplier=-1).then_inc(memset_done, 1)
            pool.affine_select(out=ident[:, :], in_=ones[:, :], compare_op=ALU.is_equal, fill=0.0, base=0,
                               pattern=[[1, P]], channel_multiplier=-1).then_inc(memset_done, 1)
            pool.affine_select(out=ident_h[:, :], in_=ones[:, :], compare_op=ALU.is_equal, fill=0.0, base=0,
                               pattern=[[1, P]], channel_multiplier=-1).then_inc(memset_done, 1)
            pool.iota(t_i[:, 0, :], [[1, TT]], base=0, channel_multiplier=TT).then_inc(memset_done, 1)

            group = pool.alloc_register("group")
            used = pool.alloc_register("used")
            landed = pool.alloc_register("landed")

            def gather(table, rows, index, done):
                for k in range(TG):
                    pool.indirect_dma_start(
                        out=rows[:, k, 0:D], out_offset=None, in_=table,
                        in_offset=bass.IndirectOffsetOnAxis(ap=index[:, k:k + 1], axis=0)).then_inc(done, 16)

            def scatter(s):
                for k in range(TG):
                    pool.indirect_dma_start(
                        out=sorted_rec, out_offset=bass.IndirectOffsetOnAxis(ap=place[s][:, k:k + 1], axis=0),
                        in_=rec[s][:, k, :], in_offset=None).then_inc(scattered[s], 16)

            def scatters(fast):
                pool.reg_mov(group, 0)
                pool.reg_mov(used, 0)
                pool.reg_mov(landed, 0)

                def one(s):
                    pool.reg_add(group, group, 1)
                    if not fast:
                        pool.wait_ge(zeroed, 16)
                        pool.wait_ge(xidx_ready, group)
                        pool.wait_ge(scattered[s], used)
                        gather(x, rec[s], gidx[s], x_gathered[s])
                        pool.wait_ge(zeroed, 16)
                        pool.wait_ge(x_gathered[s], landed)
                    pool.wait_ge(zeroed, 16)
                    pool.wait_ge(rec_ready, group)
                    pool.wait_ge(place_ready, group)
                    scatter(s)

                with pool.Fori(0, EG // 2) as i:
                    if not fast:
                        pool.reg_add(landed, landed, 16 * TG)
                    for s in range(2):
                        one(s)
                    if not fast:
                        pool.reg_add(used, used, 16 * TG)
                if not fast:
                    pool.reg_add(landed, landed, 16 * TG)
                one(0)

            pool.wait_ge(zeroed, 16 * HI)
            pool.wait_ge(prep, at["slow"])
            slow = pool.value_load(slow_i[0:1, 0:1], min_val=0, max_val=P)
            with pool.If(slow == 0):
                scatters(True)
            with pool.Else():
                scatters(False)

            def types0(g, s, n_slot, first):
                pool.wait_ge(srec0_in[s], 16 * n_slot)
                if not first:
                    pool.wait_ge(sums0, g - 1)
                for r, word in enumerate((TYP0, TYP1)):
                    ins = pool.tensor_tensor(both[s][:, :, r * D:(r + 1) * D], rec[s][:, :, 0:D],
                                             rec[s][:, :, word].unsqueeze(2).to_broadcast([P, TG, D]), ALU.mult)
                ins.then_inc(both0_ready, 1)

            for s in range(2):
                types0(s, s, 1, True)
            with pool.Fori(1, SG // 2) as i:
                for s in range(2):
                    types0(2 * i + s, s, i + 1, False)

            pool.wait_ge(att_ready, 1)
            pool.wait_ge(added0, SG + 1)
            for c in range(NC):
                hs = slice(c * C7, (c + 1) * C7)
                for r in range(2):
                    if c >= 1:
                        pool.wait_ge(n_agg, c)
                    pool.tensor_tensor(part[r][:, :, :], acc0[:, hs, r * D:(r + 1) * D],
                                       att[:, r, hs].unsqueeze(2).to_broadcast([P, C7, D]), ALU.mult).then_inc(agg_step, 1)
                pool.wait_ge(agg_step, 2 * c + 2)
                if c >= 2:
                    pool.wait_ge(n_T1, c - 1)
                pool.tensor_tensor(aggr[c % 2][:, :, 0:D], part[0][:, :, :], part[1][:, :, :], ALU.add).then_inc(n_agg, 1)

            pool.wait_ge(q_stored, 16 * NC)
            pool.wait_ge(sums0, SG)
            for s in range(2):
                pool.wait_ge(idx1_ready, s + 1)
                gather(q_table, qrow[s], gidx[s], rows1_in[s])
            pool.reg_mov(group, 2)
            pool.reg_mov(used, 0)
            with pool.Fori(1, SG // 2) as i:
                for s in range(2):
                    pool.reg_add(group, group, 1)
                    pool.reg_add(used, used, 4)
                    pool.wait_ge(q_stored, 16 * NC)
                    pool.wait_ge(idx1_ready, group)
                    pool.wait_ge(pre_added, used)
                    gather(q_table, qrow[s], gidx[s], rows1_in[s])

        @block.scalar
        def _(act):
            act.wait_ge(memset_done, 4)
            act.dma_start(by_tile[:, FULL:SS, :], zero_rec[:, :, :].to_broadcast([P, SS - FULL, R])).then_inc(tail_zeroed, 16)
            act.wait_ge(prep, at["hi"])
            for k, b in enumerate(range(B2, NB)):
                if k:
                    act.wait_ge(act_counted, k)
                act.activation(junk_act[:, :], hi_f[:, :], ACT.Sign, bias=half_b[:, b:b + 1],
                               accum_out=signs[:, b:b + 1]).then_inc(act_counted, 1)

            zero_last_tiles(act, SP_ZEROES, NC)

            def make_rec(g, s, n_slot, fast):
                act.wait_ge(attr_loaded[s], 16 * (1 if n_slot is None else n_slot + 1))
                if n_slot is not None:
                    act.wait_ge(scattered[s], 16 * TG * n_slot)
                act.activation(rec[s][:, :, D:D + A], attr_in[s][:, :, :], ACT.Copy)
                ins = act.activation(rec[s][:, :, D + A:R], meta[:, bass.ts(g, TG), :], ACT.Copy)
                if fast:
                    act.wait_ge(x_rows_done, g + 1)
                    ins = act.activation(rec[s][:, :, 0:D], banks[:, 2048 + 1024 * s:3072 + 1024 * s].rearrange("p (t d) -> p t d", d=D), ACT.Copy)
                ins.then_inc(rec_ready, 1)

            def records(fast):
                make_rec(0, 0, None, fast)
                make_rec(1, 1, None, fast)
                with act.Fori(1, EG // 2) as i:
                    for s in range(2):
                        make_rec(2 * i + s, s, i, fast)
                make_rec(EG - 1, 0, EG // 2, fast)

            act.wait_ge(prep, at["slow"])
            slow = act.value_load(slow_i[0:1, 0:1], min_val=0, max_val=P)
            with act.If(slow == 0):
                records(True)
            with act.Else():
                records(False)

            act.wait_ge(att_step, at["att"])
            for r in range(2):
                ins = act.activation(att[:, r, :], xw[:, :], ACT.Sigmoid, bias=relw[:, r:r + 1])
            ins.then_inc(att_ready, 1)

            for c in range(NC + 1):
                if c >= 1:
                    act.wait_ge(n_lin, c)
                    if c >= 2:
                        act.wait_ge(n_step, at["th", c - 2])
                    act.activation(th[:, :, :], psum[:, 2 + (c - 1) % 2, 0:C7 * D].rearrange("p (h d) -> p h d", d=D), ACT.Tanh).then_inc(n_th, 1)
                if c < NC:
                    act.wait_ge(n_T1, c + 1)
                    act.activation(nT[:, :], pair(0)[0:W], ACT.Copy).then_inc(n_T1c, 1)
            act.wait_ge(n_step, at["var"])
            act.activation(dev[:, :], var[:, :], ACT.Sqrt, bias=eps[:, :], scale=1.0 / D).then_inc(n_dev, 1)
            for c in range(NC + 1):
                if c < NC:
                    act.wait_ge(n_T2, c + 1)
                    act.activation(x1T[:, c * CW:(c + 1) * CW], pair(2 * (c % 2))[0:W], ACT.Copy).then_inc(n_T2c, 1)
                if c >= 1:
                    act.wait_ge(n_pq, c)
                    act.activation(ptab[:, (c - 1) * C7:c * C7, :], pair(4 + 2 * ((c - 1) % 2)).rearrange("p (h w) -> p h w", w=2 * D)[:, :, 0:D], ACT.Copy).then_inc(n_p, 1)

            act.wait_ge(q_stored, 16 * NC)
            for s in range(2):
                act.activation(hrow[s][:, :, D:W], ones[:, 0:TG].unsqueeze(2), ACT.Copy).then_inc(ones_set, 1)

            def edge_group(g, s, n_slot, first):
                act.wait_ge(srec1_in[s], 16 * n_slot)
                if not first:
                    act.wait_ge(attrT_done, g - 1)
                act.activation(attr_in[s][:, :, :], srec1[s][:, :, 0:A], ACT.Copy).then_inc(attr_packed, 1)
                act.wait_ge(attrT_done, g + 1)
                if not first:
                    act.wait_ge(pre_done, 4 * (g - 1))
                act.activation(attrT[s], psum[:, 5, :].rearrange("p (q e) -> p q e", e=P), ACT.Copy).then_inc(attrT_copied, 1)
                for q in range(4):
                    act.wait_ge(hotT_done, 4 * g + q + 1)
                    if not (first and s == 0):
                        act.wait_ge(pre_done, 4 * g + q - 3)
                    act.activation(hotT[:, 4 * q:4 * q + 4, :], psum[:, 3 + q % 2, :].rearrange("p (t e) -> p t e", e=P), ACT.Copy).then_inc(hotT_copied, 1)
                for q in range(4):
                    act.wait_ge(pre_added, 4 * g + q + 1)
                    if not first and q == 0:
                        act.wait_ge(sums1, g - 1)
                    act.activation(hrow[s][:, 4 * q:4 * q + 4, 0:D], pre[s][:, 4 * q:4 * q + 4, :], ACT.Relu).then_inc(h_ready, 1)

            for s in range(2):
                edge_group(s, s, 1, True)
            with act.Fori(1, SG // 2) as i:
                for s in range(2):
                    edge_group(2 * i + s, s, i + 1, False)

            act.wait_ge(sums1, SG)
            act.activation(hidT[D:W, :], x1T[D:W, 0:CW], ACT.Copy).then_inc(ones_set, 1)
            for c in range(NC + 2):
                if 0 <= c - 2 < NC:
                    act.wait_ge(f_hid, c - 1)
                    act.activation(hidT[0:D].rearrange("p (b n) -> p b n", b=2), psum[0:D, 4:6, 0:CW // 2], ACT.Relu).then_inc(f_hidc, 1)
                if 0 <= c - 1 < NC:
                    act.wait_ge(f_ag, c)
                    act.activation(agT.rearrange("p (b n) -> p b n", b=2), psum[0:D, 2:4, 0:CW // 2], ACT.Copy).then_inc(f_agc, 1)
                if c < NC:
                    act.wait_ge(f_T, c + 1)
                    act.activation(hT, pair(0)[0:W], ACT.Copy).then_inc(f_Tc, 1)
            act.wait_ge(f_step, at["var1"])
            act.activation(dev[:, :], var[:, :], ACT.Sqrt, bias=eps[:, :], scale=1.0 / D).then_inc(f_dev, 1)

        @block.tensor
        def _(pe):
            pe.wait_ge(memset_done, MEMSETS)
            pe.wait_ge(prep, at["count"])
            pe.matmul(psum[:, 0, 0:NB], lower[:, :], count[:, :], start=True, stop=True)
            pe.matmul(psum[:, 0, 64:64 + NB], ones[:, :], count[:, :], start=True, stop=True).then_inc(sums_ready, 1)
            pe.wait_ge(prep, at["meta"])
            pe.matmul(psum[:, 1, 0:EG], first_row[:, :],
                      meta[:, :, 1].rearrange("p (g k) -> p g k", k=TG)[:, :, 0], start=True, stop=True).then_inc(sums_ready, 1)
            pe.wait_ge(prep, at["outside"])
            pe.matmul(psum[:, 2, 0:1], ones[:, :], outside[:, :], start=True, stop=True).then_inc(sums_ready, 1)

            def dst_rows(g, s, first=False):
                if not first:
                    pe.wait_ge(win_hot_ready, g - 1)
                for k in range(TG):
                    ins = pe.transpose(win_T[s][:, k * P:(k + 1) * P],
                                       in_win[:, bass.ds(g * TG + k, 1)].to_broadcast([P, P]), ident_h[:, :])
                ins.then_inc(dstT_done, 1)

            def x_rows(g, s, n_slot):
                pe.wait_ge(win_hot_ready, g + 1)
                pe.wait_ge(split_step, (g + 1) * SPLIT_STEPS)
                if n_slot is not None:
                    pe.wait_ge(rec_ready, g - 1)
                for k in range(TG):
                    for n in range(6):
                        ins = pe.matmul(banks[:, 2048 + 1024 * s + k * D:2048 + 1024 * s + (k + 1) * D],
                                        win_hot[s][:, n // 3, k * P:(k + 1) * P], xpart[s][:, n % 3, n // 3, :],
                                        start=(n == 0), stop=(n == 5))
                ins.then_inc(x_rows_done, 1)

            pe.wait_ge(prep, at["slow"])
            slow = pe.value_load(slow_i[0:1, 0:1], min_val=0, max_val=P)
            with pe.If(slow == 0):
                dst_rows(0, 0, True)
                dst_rows(1, 1, True)
                x_rows(0, 0, None)
                dst_rows(2, 0)
                x_rows(1, 1, None)
                with pe.Fori(1, EG // 2) as i:
                    for s in range(2):
                        dst_rows(2 * i + s + 1, 1 - s)
                        x_rows(2 * i + s, s, i)
                x_rows(EG - 1, 0, EG // 2)
            with pe.Else():
                pe.nop()

            slot_regs = [pe.alloc_register(f"slot{k}") for k in range(TG)]
            hi_regs = [pe.alloc_register(f"hi{k}") for k in range(TG)]

            def load_tiles(regs, table, g, top):
                pe.load(regs, table[0:1, bass.ts(g, TG)])
                return [pe.snap(r, min_val=0, max_val=top) for r in regs]

            def sums_of_group0(g, s, first):
                slots = load_tiles(slot_regs, tile_slot, g, SLOTS - 1)
                if not first:
                    pe.wait_ge(added0, g)
                for b in range(4):
                    pe.matmul(psum[:, 4 * s + b, :], zeros[:, 0:P], zeros[:, :], start=True, stop=False, skip_group_check=True)
                pe.wait_ge(hot0_ready, g + 1)
                pe.wait_ge(both0_ready, g + 1)
                for k in range(TG):
                    ins = pe.matmul(banks[:, 2048 * s:2048 * s + 2048][:, bass.ts(slots[k], 2 * D)], hot[s][:, k, :], both[s][:, k, :],
                                    start=False, stop=True, skip_group_check=True)
                ins.then_inc(sums0, 1)

            pe.wait_ge(table_in, 32)
            for s in range(2):
                sums_of_group0(s, s, True)
            with pe.Fori(1, SG // 2) as i:
                for s in range(2):
                    sums_of_group0(2 * i + s, s, False)

            pe.wait_ge(node_in, 16 * 21)
            pe.wait_ge(added0, SG + 1)
            for c in range(NC + 1):
                if c >= 1:
                    pe.wait_ge(n_T1c, c)
                    if c >= 3:
                        pe.wait_ge(n_th, c - 2)
                    for h in range(C7):
                        ins = pe.matmul(psum[:, 2 + (c - 1) % 2, h * D:(h + 1) * D], nT[:, h * P:(h + 1) * P], W65[:, :], start=True, stop=True)
                    ins.then_inc(n_lin, 1)
                if c < NC:
                    pe.wait_ge(n_agg, c + 1)
                    for h in range(C7):
                        ins = pe.transpose(banks[0:W, h * P:(h + 1) * P], aggr[c % 2][:, h, :], ident[:, :])
                    ins.then_inc(n_T1, 1)
            pe.wait_ge(n_th, NC)
            for c in range(NC + 1):
                if c < NC:
                    pe.wait_ge(n_x1, c + 1)
                    if c >= 2:
                        pe.wait_ge(n_T2c, c - 1)
                    for h in range(C7):
                        ins = pe.transpose(pair(2 * (c % 2))[0:W, h * P:(h + 1) * P], x1[:, c * C7 + h, :], ident[:, :])
                    ins.then_inc(n_T2, 1)
                if c >= 1:
                    pe.wait_ge(n_T2c, c)
                    if c >= 3:
                        pe.wait_ge(n_p, c - 2)
                        pe.wait_ge(n_q, c - 2)
                    for h in range(C7):
                        t = (c - 1) * C7 + h
                        ins = pe.matmul(pair(4 + 2 * ((c - 1) % 2))[:, h * P:(h + 1) * P], x1T[:, t * P:(t + 1) * P], Eab[:, :], start=True, stop=True)
                    ins.then_inc(n_pq, 1)
            pe.wait_ge(n_q, NC)
            pe.wait_ge(n_p, NC)

            ptab_w = merged(ptab[:, :, :])

            def slot_at(v):
                return v * W + (v // L1B) * (512 - L1B * W)

            def edge_group(g, s, n_slot, first):
                slots = load_tiles(slot_regs, tile_slot, g, SLOTS - 1)
                his = load_tiles(hi_regs, tile_hi, g, HI - 1)
                pe.wait_ge(attr_packed, g + 1)
                if not (first and s == 0):
                    pe.wait_ge(attrT_copied, g)
                packed = merged(attr_in[s][:, :, :])
                for q in range(4):
                    ins = pe.transpose(psum[:, 5, q * P:(q + 1) * P], packed[:, 4 * A * q:4 * A * (q + 1)], ident[:, :])
                ins.then_inc(attrT_done, 1)
                pe.wait_ge(hot1_ready, g + 1)

                def transpose_hot(q):
                    if not (first and s == 0 and q < 2):
                        pe.wait_ge(hotT_copied, 4 * g + q - 1)
                    for k in range(4):
                        ins = pe.transpose(psum[:, 3 + q % 2, k * P:(k + 1) * P], hot[s][:, 4 * q + k, :], ident[:, :])
                    ins.then_inc(hotT_done, 1)

                def values(q):
                    if q == 0:
                        pe.wait_ge(attrT_copied, g + 1)
                    if not (first and s == 0 and q < 2):
                        pe.wait_ge(pre_added, 4 * g + q - 1)
                    bank = psum[:, 6 + q % 2, 0:4 * D]
                    pe.matmul(bank, attrT[s][:, q, :], merged(ec_blk[:, :, :]), start=True, stop=False, skip_group_check=True)
                    pe.wait_ge(hotT_copied, 4 * g + q + 1)
                    for k in range(4):
                        ins = pe.matmul(bank[:, k * D:(k + 1) * D], hotT[:, 4 * q + k, :],
                                        ptab_w[:, bass.ts(his[4 * q + k], D)], start=False, stop=True, skip_group_check=True)
                    ins.then_inc(pre_done, 1)

                transpose_hot(0)
                transpose_hot(1)
                values(0)
                transpose_hot(2)
                values(1)
                transpose_hot(3)
                values(2)
                values(3)
                if not (first and s == 0):
                    pe.wait_ge(added1, g + 1)
                for b in range(3):
                    pe.matmul(psum[:, b, :], zeros[:, 0:P], zeros[:, :], start=True, stop=False, skip_group_check=True)
                for k in range(TG):
                    if k % 4 == 0:
                        pe.wait_ge(h_ready, 4 * g + k // 4 + 1)
                    ins = pe.matmul(banks[:, bass.ds(slot_at(slots[k]), W)], hot[s][:, k, :], hrow[s][:, k, :],
                                    start=False, stop=True, skip_group_check=True)
                ins.then_inc(sums1, 1)

            pe.wait_ge(ones_set, 2)
            for s in range(2):
                edge_group(s, s, 1, True)
            with pe.Fori(1, SG // 2) as i:
                for s in range(2):
                    edge_group(2 * i + s, s, i + 1, False)

            pe.wait_ge(ones_set, 3)
            pe.wait_ge(added1, SG + 1)
            H = CW // 2
            for c in range(NC + 3):
                if 0 <= c - 3 < NC:
                    k = c - 3
                    pe.wait_ge(f_hidc, k + 1)
                    if k >= 2:
                        pe.wait_ge(f_step, at["out", k - 2])
                    for h in range(C7):
                        ins = pe.matmul(psum[:, 6 + k % 2, h * D:(h + 1) * D], hidT[:, h * P:(h + 1) * P], nw2_65[:, :], start=True, stop=True)
                    ins.then_inc(f_out, 1)
                if 0 <= c - 2 < NC:
                    k = c - 2
                    pe.wait_ge(f_agc, k + 1)
                    if k >= 1:
                        pe.wait_ge(f_hidc, k)
                    for b in range(2):
                        pe.matmul(psum[0:D, 4 + b, 0:H], na65[:, :], x1T[:, k * CW + b * H:k * CW + (b + 1) * H], start=True, stop=False)
                        ins = pe.matmul(psum[0:D, 4 + b, 0:H], nb64[:, :], agT[:, b * H:(b + 1) * H], start=False, stop=True)
                    ins.then_inc(f_hid, 1)
                if 0 <= c - 1 < NC:
                    k = c - 1
                    pe.wait_ge(f_Tc, k + 1)
                    if k >= 1:
                        pe.wait_ge(f_agc, k)
                    for b in range(2):
                        ins = pe.matmul(psum[0:D, 2 + b, 0:H], ew2_65[:, :], hT[:, b * H:(b + 1) * H], start=True, stop=True)
                    ins.then_inc(f_ag, 1)
                if c < NC:
                    if c >= 1:
                        pe.wait_ge(f_Tc, c)
                    for h in range(C7):
                        ins = pe.transpose(banks[0:W, h * P:(h + 1) * P], acc1[:, c * C7 + h, :], ident[:, :])
                    ins.then_inc(f_T, 1)


SP_ZEROES = 3
MEMSETS = 21


_INS = ["x", "src", "dst", "edge_attr_32", "edge_type_2", "L0_gnn_relation_emb", "L0_gnn_att_w", "L0_gnn_att_b",
        "L0_gnn_W_wT", "L0_gnn_W_b", "L1_gnn_ew1", "L1_gnn_eb1", "L1_gnn_ew2", "L1_gnn_eb2", "L1_gnn_nw1",
        "L1_gnn_nb1", "L1_gnn_nw2", "L1_gnn_nb2"]


def kernel(**inputs):
    import numpy as np
    import concourse.bacc as bacc
    from concourse.bass_utils import run_bass_kernel_spmd

    inputs["L0_gnn_W_wT"] = np.asarray(inputs["L0_gnn_W_w"]).T
    nc = bacc.Bacc("TRN2", target_bir_lowering=False, num_devices=1)
    arrays, args = {}, []
    for name in _INS:
        a = np.ascontiguousarray(inputs[name])
        arrays[f"in_{name}"] = a
        args.append(nc.dram_tensor(f"in_{name}", a.shape, mybir.dt.from_np(a.dtype), kind="ExternalInput").ap())
    out = nc.dram_tensor("out_nodes", (N, D), f32, kind="ExternalOutput").ap()
    bass_gnn_two_layers(nc, *args, out)
    r = run_bass_kernel_spmd(nc, [arrays], core_ids=[0])
    return r.results[0]["out_nodes"]
```

```python
import concourse.bass as bass
from concourse import mybir
from contextlib import ExitStack

f32 = mybir.dt.float32
i32 = mybir.dt.int32
bf16 = mybir.dt.bfloat16
ALU = mybir.AluOpType
ACT = mybir.ActivationFunctionType
AX = mybir.AxisListType

N = 6250
E = 100000
D = 64
A = 32
P = 128
HI = -(-N // P)
TG = 16
GE = TG * P
EG = -(-E // GE)
EJ = EG * TG
TAIL = (E - (EG - 1) * GE) // TG
WIN = 2 * P
NB = HI + 1
B2 = 7 * NB // 10
ST = 832
SG = ST // TG
SS = ST + TG
FULL = E // P
META = 3
R = D + A + META
KEY, DST, TYP = range(D + A, R)
TT = 7
C7 = 7
NC = HI // C7
W = D + 1
SLOTS = TG
HALF = SLOTS * D
AHEAD = 4
HOT_POOL = 4
L1B = 7
RANK_STEPS = 8
SPLIT_STEPS = 4
EPS = 1e-05
assert (EG - 1) * GE + TAIL * TG == E and HI == C7 * NC and TT * P >= ST
assert (E + (P - 1) * HI + HI) // P <= ST and EG % 2 == 1 and SG % 2 == 0
assert SG % AHEAD == 0 and 2 * TG * R <= 5 * EJ and HI * P == 8 * EJ and FULL * P <= E and ST - FULL >= 0


def bass_gnn_two_layers(nc, x, src, dst, attr, etype, rel, att_w, att_b, WT, W_b,
                        ew1, eb1, ew2, eb2, nw1, nb1, nw2, nb2, out):
    sorted_rec = nc.dram_tensor("sorted_rec", (P * SS, R), f32, kind="Internal").ap()
    q_table = nc.dram_tensor("q_table", (HI * P, D), f32, kind="Internal").ap()
    tile_dram = nc.dram_tensor("tile_dram", (2, TT * P), i32, kind="Internal").ap()
    by_tile = sorted_rec.rearrange("(p t) r -> p t r", p=P)
    by_lane = sorted_rec.rearrange("(p t) r -> p (t r)", p=P)

    ctx = ExitStack()
    with ctx:
        def sb(name, shape, dt=f32):
            return ctx.enter_context(nc.sbuf_tensor(name, shape, dt))

        def sem(name):
            return ctx.enter_context(nc.semaphore(name))

        def sems(name, n):
            return [sem(f"{name}{k}") for k in range(n)]

        def merged(ap):
            return ap.rearrange("p a b -> p (a b)")

        early = sb("early", [P, 8 * EJ])
        src_i, dst_i, typ_i = (early[:, n * EJ:(n + 1) * EJ].bitcast(i32).rearrange("p (g k) -> p g k", k=TG) for n in range(3))
        lo_i = early[:, 3 * EJ:4 * EJ].bitcast(i32)
        meta = early[:, 4 * EJ:(4 + META) * EJ].rearrange("p (j r) -> p j r", r=META)
        hi_f = sb("hi_f", [P, EJ])
        attr_in = [sb(f"attr_in{s}", [P, TG, A]) for s in range(2)]
        rec = [sb(f"rec{s}", [P, TG, R]) for s in range(2)]
        place = [sb(f"place{s}", [P, TG], i32) for s in range(2)]
        xwin = [sb(f"xwin{s}", [P, 2, D]) for s in range(2)]
        xpart = [sb(f"xpart{s}", [P, 3, 2, D], bf16) for s in range(2)]
        xrest = sb("xrest", [P, 2, D])
        win_base = sb("win_base", [P, EG])
        in_win = sb("in_win", [P, EJ], bf16)
        win_i = sb("win_i", [P, EG], i32)
        far = sb("far", [P, 1])
        outside = sb("outside", [P, 1])
        slow_i = sb("slow_i", [P, 1], i32)
        full_i = sb("full_i", [P, 1], i32)
        count = sb("count", [P, NB])
        signs = sb("signs", [P, NB])
        half_b = sb("half_b", [P, NB])
        iota_b = sb("iota_b", [P, NB])
        iota_w = sb("iota_w", [P, 2])
        lower = sb("lower", [P, P])
        first_row = sb("first_row", [P, P])
        ones = sb("ones", [P, P])
        before = sb("before", [P, NB])
        total = sb("total", [P, NB])
        tiles_i = sb("tiles_i", [P, NB], i32)
        tiles_j = sb("tiles_j", [P, NB], i32)
        tiles_f = sb("tiles_f", [P, NB])
        tile_end = sb("tile_end", [P, NB])
        ends_i = sb("ends_i", [P, NB], i32)
        reset = sb("reset", [P, NB, TG + 1])
        marks = sb("marks", [P, NB, TG + 1])
        ranks = sb("ranks", [P, NB, TG + 1])
        picked = sb("picked", [P, NB, TG])
        off = picked[:, 0:EG, :]
        base = sb("base", [P, NB])
        pos_f = sb("pos_f", [P, TG])
        pos_i = sb("pos_i", [P, TG], i32)
        pos_j = sb("pos_j", [P, TG], i32)
        pos_k = sb("pos_k", [P, TG], i32)
        t_i = sb("t_i", [P, 2, TT], i32)
        t_f = sb("t_f", [P, 2, TT])
        t_cmp = merged(ranks[:, :, :])[:, 0:2 * TT * (HI - 1)].rearrange("p (t b) -> p t b", b=HI - 1)
        t_hi = sb("t_hi", [P, 2, TT])
        t_slot = sb("t_slot", [P, TT])
        t_out = sb("t_out", [P, 2, TT], i32)
        tile_hi = sb("tile_hi", [1, TT * P], i32)
        tile_slot = sb("tile_slot", [1, TT * P], i32)
        gidx = [sb(f"gidx{s}", [P, TG], i32) for s in range(2)]
        iota_lo = sb("iota_lo", [P, P])
        ident = sb("ident", [P, P])
        ident_h = sb("ident_h", [P, P], bf16)
        hot_all = sb("hot_all", [P, 2, TG * P])
        hot = [hot_all[:, s, :].rearrange("p (t e) -> p t e", e=P) for s in range(2)]
        win_hot = [hot_all[:, s, :].bitcast(bf16).rearrange("p (w e) -> p w e", w=2) for s in range(2)]
        both = [sb(f"both{s}", [P, TG, 2 * D]) for s in range(2)]
        zeros = sb("zeros", [P, 512], bf16)
        zero_rec = sb("zero_rec", [P, 1, R])
        acc0 = sb("acc0", [P, HI + SLOTS, 2 * D])
        junk_dve, junk_act, hi_h = (merged(acc0[:, 8 * n:8 * n + 4, :]).bitcast(bf16)[:, 0:EJ] for n in range(3))
        xs = sb("xs", [P, HI, D])
        att = sb("att", [P, 2, HI])
        xw = sb("xw", [P, HI])
        wide = sb("wide", [P, 2, D])
        relw = sb("relw", [P, 2])
        attw_b = sb("attw_b", [P, 2, D])
        attb_b = sb("attb_b", [P, 1])
        rel_b = sb("rel_b", [P, 2, D])
        W65 = sb("W65", [W, D])
        Eab = sb("Eab", [W, 2 * D])
        ec_blk = sb("ec_blk", [P, 4, D])
        ew2_65 = sb("ew2_65", [W, D])
        na65 = sb("na65", [W, D])
        nb64 = sb("nb64", [D, D])
        ew2T = sb("ew2T", [D, W])
        M65 = sb("M65", [W, D])
        nw2_65 = sb("nw2_65", [W, D])
        x1 = sb("x1", [P, HI, W])
        x1T = early[0:W, :]
        ptab = sb("ptab", [P, HI, D])
        acc1 = sb("acc1", [P, HI + 3 * L1B, W])
        aggr = [sb(f"aggr{s}", [P, C7, W]) for s in range(2)]
        part = [hot_all[:, 0, r * C7 * D:(r + 1) * C7 * D].rearrange("p (h d) -> p h d", d=D) for r in range(2)]
        th = [merged(both[s][:, 0:4, :])[:, 0:C7 * D].rearrange("p (h d) -> p h d", d=D) for s in range(2)]
        tmp = merged(both[0][:, 4:8, :])[:, 0:C7 * D].rearrange("p (h d) -> p h d", d=D)
        mean = sb("mean", [P, C7])
        var = [sb(f"var{s}", [P, C7]) for s in range(2)]
        power = sb("power", [P, C7])
        rstd = [sb(f"rstd{s}", [P, C7]) for s in range(2)]
        srec0 = [rec[s][:, :, :] if s < 2 else early[:, (s - 2) * TG * R:(s - 1) * TG * R].rearrange("p (t r) -> p t r", r=R)
                 for s in range(AHEAD)]
        srec1 = [merged(rec[s][:, :, :])[:, 0:TG * (A + META)].rearrange("p (t r) -> p t r", r=A + META) for s in range(2)]
        qrow = [merged(both[s][:, 0:8, :]).rearrange("p (t d) -> p t d", d=D) for s in range(2)]
        pre = [merged(both[s][:, 8:16, :]).rearrange("p (t d) -> p t d", d=D) for s in range(2)]
        attrT = [acc0[:, 8 * s:8 * s + 4, :] for s in range(2)]
        hrow = [merged(acc0[:, 16 + 10 * s:16 + 10 * s + 9, :])[:, 0:TG * W].rearrange("p (t w) -> p t w", w=W) for s in range(2)]
        hotT = acc0[:, 36:52, :]
        q_out = merged(acc0[:, 0:25, :])[:, 0:HI * D].rearrange("p (h d) -> p h d", d=D)
        hidT, nT = ([hot_all[0:W, n, 8 * P * s:8 * P * s + C7 * P] for s in range(2)] for n in range(2))

        psum = ctx.enter_context(nc.psum_tensor("psum", [P, 8, 512], f32))
        banks = psum[:, :, :].rearrange("p b n -> p (b n)")
        win_T = [banks[:, 1024 * s:1024 * (s + 1)].bitcast(bf16) for s in range(2)]
        CW = C7 * P
        pair = lambda b: banks[:, 512 * b:512 * b + CW]

        src_loaded = sem("src_loaded")
        loaded = sem("loaded")
        node_in = sem("node_in")
        memset_done = sem("memset_done")
        tail_zeroed = sem("tail_zeroed")
        zeroed = sem("zeroed")
        zeroed_pool = sem("zeroed_pool")
        prep = sem("prep")
        act_counted = sem("act_counted")
        sums_ready = sem("sums_ready")
        table_out = sem("table_out")
        table_in = sem("table_in")
        attr_loaded = sems("attr_loaded", 2)
        xwin_in = sems("xwin_in", 2)
        split_step = sem("split_step")
        dstT_done = sem("dstT_done")
        win_hot_ready = sem("win_hot_ready")
        x_rows_done = sem("x_rows_done")
        xidx_ready = sem("xidx_ready")
        x_gathered = sems("x_gathered", 2)
        rec_ready = sem("rec_ready")
        place_ready = sem("place_ready")
        rank_step = sem("rank_step")
        scattered = sems("scattered", 2)
        att_step = sem("att_step")
        att_ready = sem("att_ready")
        srec0_in = sems("srec0_in", AHEAD)
        hot0_ready = sem("hot0_ready")
        x0_copied = sem("x0_copied")
        cleared0 = sem("cleared0")
        both0_ready = sem("both0_ready")
        sums0 = sem("sums0")
        added0 = sem("added0")
        agg_step = sem("agg_step")
        n_agg = sem("n_agg")
        n_T1 = sem("n_T1")
        n_T1c = sem("n_T1c")
        n_lin = sem("n_lin")
        n_th = sem("n_th")
        n_step = sem("n_step")
        n_rstd = sem("n_rstd")
        n_x1 = sem("n_x1")
        n_T2 = sem("n_T2")
        n_T2c = sem("n_T2c")
        n_pq = sem("n_pq")
        n_p = sem("n_p")
        n_q = sem("n_q")
        q_stored = sem("q_stored")
        srec1_in = sems("srec1_in", 2)
        idx1_ready = sem("idx1_ready")
        rows1_in = [sems(f"rows1_in{s}_", 2) for s in range(2)]
        hot1_ready = sem("hot1_ready")
        attr_packed = sem("attr_packed")
        attrT_done = sem("attrT_done")
        attrT_copied = sem("attrT_copied")
        hotT_done = sem("hotT_done")
        hotT_copied = sem("hotT_copied")
        pre_done = sem("pre_done")
        pre_added = sem("pre_added")
        h_ready = sem("h_ready")
        sums1 = sem("sums1")
        added1 = sem("added1")
        ones_set = sem("ones_set")
        w_step = sem("w_step")
        w_copied = sem("w_copied")
        x_lin = sem("x_lin")
        x_linc = sem("x_linc")
        f_T = sem("f_T")
        f_Tc = sem("f_Tc")
        f_sum = sem("f_sum")
        f_hid = sem("f_hid")
        f_hidc = sem("f_hidc")
        f_out = sem("f_out")
        f_step = sem("f_step")
        f_rstd = sem("f_rstd")
        f_ready = sem("f_ready")
        stored = sem("stored")

        at = {}
        block = ctx.enter_context(nc.Block())

        def zero_last_tiles(eng, start, stop, done):
            eng.wait_ge(prep, at["ends"])
            eng.wait_ge(tail_zeroed, 16)
            ends = [eng.alloc_register(f"end{k}") for k in range(C7)]
            with eng.Fori(start, stop) as i:
                eng.load(ends, ends_i[0:1, bass.ts(i, C7)])
                for k in range(C7):
                    end = eng.snap(ends[k], min_val=0, max_val=ST - 1)
                    eng.dma_start(by_tile[:, bass.ds(end, 1), :], zero_rec[:, :, :]).then_inc(done, 16)

        def last_group_flag(eng):
            return eng.value_load(full_i[0:1, 0:1], min_val=0, max_val=1)

        @block.vector
        def _(dve):
            def chain(semaphore, start=0):
                n = [0]

                def step(ins):
                    n[0] += 1
                    ins.then_inc(semaphore, 1)
                    dve.wait_ge(semaphore, start + n[0])
                return step, n

            step, n = chain(prep)
            dve.wait_ge(memset_done, 6)
            step(dve.tensor_scalar(half_b[:, :], iota_b[:, :], -1.0, 0.5, ALU.mult, ALU.add))
            dve.wait_ge(src_loaded, 32)
            src2, dst2, typ2 = merged(src_i), merged(dst_i), merged(typ_i)
            step(dve.tensor_scalar(lo_i, src2, 7, None, ALU.logical_shift_right))
            step(dve.tensor_copy(hi_f[:, :], lo_i))
            at["hi"] = n[0]
            step(dve.tensor_copy(hi_h[:, :], hi_f[:, :]))
            for b in range(B2):
                step(dve.tensor_scalar(junk_dve[:, :], hi_h[:, :], float(b), None, ALU.is_equal, ALU.add,
                                       accum_out=count[:, b:b + 1]))
            dve.wait_ge(act_counted, NB - B2)
            step(dve.tensor_tensor(count[:, B2:NB - 1], signs[:, B2:NB - 1], signs[:, B2 + 1:NB], ALU.subtract))
            step(dve.tensor_scalar(count[:, B2:NB - 1], count[:, B2:NB - 1], 0.5, None, ALU.mult))
            step(dve.tensor_scalar(count[:, NB - 1:NB], signs[:, NB - 1:NB], 0.5, EJ / 2, ALU.mult, ALU.add))
            at["count"] = n[0]
            dve.wait_ge(sums_ready, 1)
            step(dve.tensor_copy(total[:, :], psum[:, 0, 64:64 + NB]))
            step(dve.tensor_scalar(tiles_i[:, :], total[:, :], float(P - 1), float(P), ALU.add, ALU.max))
            step(dve.tensor_scalar(tiles_j[:, :], tiles_i[:, :], 7, None, ALU.logical_shift_right))
            step(dve.tensor_copy(tiles_f[:, :], tiles_j[:, :]))
            step(dve.tensor_tensor_scan(tile_end[:, :], tiles_f[:, :], ones[:, 0:NB], 0.0, ALU.add, ALU.mult))
            step(dve.tensor_scalar(ends_i[:, :], tile_end[:, :], -1.0, None, ALU.add))
            at["ends"] = n[0]
            step(dve.tensor_scalar(full_i[:, :], tile_end[:, HI - 1:HI], float(ST - TG), None, ALU.is_gt))
            dve.wait_ge(loaded, 64)
            step(dve.tensor_copy(meta[:, :, 1], dst2))
            at["dst"] = n[0]
            dve.wait_ge(sums_ready, 2)
            step(dve.tensor_scalar(win_base[:, :], psum[:, 1, 0:EG], float(N - WIN), None, ALU.min))
            step(dve.tensor_copy(win_i[:, :], win_base[:, :]))
            at["windows"] = n[0]
            step(dve.tensor_tensor(off[:, :, :], meta[:, :, 1].rearrange("p (g k) -> p g k", k=TG),
                                   win_base[:, :].unsqueeze(2).to_broadcast([P, EG, TG]), ALU.subtract))
            step(dve.tensor_copy(in_win[:, :], merged(off[:, :, :])))
            step(dve.tensor_scalar(off[:, :, :], off[:, :, :], -(WIN - 1) / 2, None, ALU.add))
            step(dve.tensor_tensor(off[:, :, :], off[:, :, :], off[:, :, :], ALU.mult))
            step(dve.tensor_reduce(far[:, :], merged(off[:, :, :]), AX.X, ALU.max))
            step(dve.tensor_scalar(outside[:, :], far[:, :], float(P * P), None, ALU.is_ge))
            at["outside"] = n[0]
            step(dve.tensor_copy(before[:, :], psum[:, 0, 0:NB]))
            step(dve.tensor_scalar(lo_i, src2, P - 1, None, ALU.bitwise_and))
            step(dve.tensor_scalar(meta[:, :, 0], lo_i, 1, None, ALU.add))
            step(dve.tensor_copy(meta[:, :, 2], typ2))
            at["meta"] = n[0]
            step(dve.tensor_tensor(base[:, :], tile_end[:, :], tiles_f[:, :], ALU.subtract))
            step(dve.memset(base[:, HI:NB], float(ST)))
            step(dve.tensor_scalar(base[:, :], base[:, :], float(P), None, ALU.mult))
            step(dve.tensor_tensor(marks[:, :, 0], base[:, :], before[:, :], ALU.add))
            dve.wait_ge(sums_ready, 3)
            step(dve.tensor_copy(slow_i[:, :], psum[:, 2, 0:1]))
            at["slow"] = n[0]

            def rank(g, s, n_slot):
                m = [0]

                def rstep(ins):
                    m[0] += 1
                    ins.then_inc(rank_step, 1)
                    dve.wait_ge(rank_step, g * RANK_STEPS + m[0])
                rstep(dve.tensor_tensor(marks[:, :, 1:TG + 1], hi_f[:, bass.ts(g, TG)].unsqueeze(1).to_broadcast([P, NB, TG]),
                                        iota_b[:, :].unsqueeze(2).to_broadcast([P, NB, TG]), ALU.is_equal))
                rstep(dve.tensor_tensor_scan(merged(ranks[:, :, :]), merged(reset[:, :, :]), merged(marks[:, :, :]),
                                             0.0, ALU.mult, ALU.add))
                rstep(dve.tensor_tensor(picked[:, :, :], marks[:, :, 1:TG + 1], ranks[:, :, 1:TG + 1], ALU.mult))
                rstep(dve.tensor_copy(marks[:, :, 0], ranks[:, :, TG]))
                rstep(dve.tensor_reduce(pos_f[:, :], picked[:, :, :].rearrange("p b k -> p k b"), AX.X, ALU.add))
                rstep(dve.tensor_scalar(pos_i[:, :], pos_f[:, :], -1.0, None, ALU.add))
                rstep(dve.tensor_scalar(pos_j[:, :], pos_i[:, :], P - 1, None, ALU.bitwise_and))
                rstep(dve.tensor_scalar(pos_k[:, :], pos_i[:, :], 7, None, ALU.logical_shift_right))
                if n_slot is not None:
                    dve.wait_ge(scattered[s], 16 * TG * n_slot)
                dve.scalar_tensor_tensor(place[s][:, :], pos_j[:, :], float(SS), pos_k[:, :], ALU.mult, ALU.add).then_inc(place_ready, 1)
                assert m[0] == RANK_STEPS

            def window_matrices(g, s, n_slot):
                dve.wait_ge(dstT_done, g + 1)
                if n_slot is not None:
                    dve.wait_ge(x_rows_done, g - 1)
                for w in range(2):
                    ins = dve.tensor_scalar(win_hot[s][:, w, :], win_T[s], iota_w[:, w:w + 1], None, ALU.is_equal)
                ins.then_inc(win_hot_ready, 1)

            def split_window(g, s, n_slot):
                m = [0]

                def sstep(ins):
                    m[0] += 1
                    ins.then_inc(split_step, 1)
                    dve.wait_ge(split_step, g * SPLIT_STEPS + m[0])
                dve.wait_ge(xwin_in[s], 16 * (1 if n_slot is None else n_slot + 1))
                hi, mid, lo = (xpart[s][:, k, :, :] for k in range(3))
                sstep(dve.tensor_copy(hi, xwin[s][:, :, :]))
                sstep(dve.tensor_tensor(xrest[:, :, :], xwin[s][:, :, :], hi, ALU.subtract))
                sstep(dve.tensor_copy(mid, xrest[:, :, :]))
                sstep(dve.tensor_tensor(lo, xrest[:, :, :], mid, ALU.subtract))
                assert m[0] == SPLIT_STEPS

            def indices(g, s, n_slot):
                if n_slot is not None:
                    dve.wait_ge(x_gathered[s], 16 * TG * n_slot)
                dve.tensor_copy(gidx[s][:, :], meta[:, bass.ts(g, TG), 1]).then_inc(xidx_ready, 1)

            def places(fast):
                def group(g, s, n_slot):
                    if fast:
                        window_matrices(g, s, n_slot)
                        split_window(g, s, n_slot)
                    else:
                        indices(g, s, n_slot)
                    rank(g, s, n_slot)
                group(0, 0, None)
                group(1, 1, None)
                with dve.Fori(1, EG // 2) as i:
                    for s in range(2):
                        group(2 * i + s, s, i)
                group(EG - 1, 0, EG // 2)

            slow = dve.value_load(slow_i[0:1, 0:1], min_val=0, max_val=P)
            with dve.If(slow == 0):
                places(True)
            with dve.Else():
                places(False)

            step, n = chain(prep, n[0])
            before_table = at["slow"]
            dve.wait_ge(memset_done, MEMSETS)
            step(dve.tensor_scalar(t_i[:, 1, :], t_i[:, 0, :], 4, 4, ALU.logical_shift_right, ALU.logical_shift_left))
            step(dve.tensor_copy(t_f[:, :, :], t_i[:, :, :]))
            step(dve.tensor_tensor(t_cmp[:, :, :], merged(t_f[:, :, :]).unsqueeze(2).to_broadcast([P, 2 * TT, HI - 1]),
                                   tile_end[:, 0:HI - 1].unsqueeze(1).to_broadcast([P, 2 * TT, HI - 1]), ALU.is_ge))
            step(dve.tensor_reduce(merged(t_hi[:, :, :]), t_cmp[:, :, :], AX.X, ALU.add))
            step(dve.tensor_tensor(t_slot[:, :], t_hi[:, 0, :], t_hi[:, 1, :], ALU.subtract))
            step(dve.tensor_copy(t_out[:, 0, :], t_hi[:, 0, :]))
            step(dve.tensor_copy(t_out[:, 1, :], t_slot[:, :]))
            at["table"] = before_table + n[0]

            dve.wait_ge(node_in, 16 * 21)
            step, n = chain(att_step)
            big = acc0[:, 0:HI, 0:D]
            step(dve.tensor_tensor(big, xs[:, :, :], attw_b[:, 0, :].unsqueeze(1).to_broadcast([P, HI, D]), ALU.mult))
            step(dve.tensor_reduce(xw[:, :], big, AX.X, ALU.add))
            step(dve.tensor_tensor(wide[:, :, :], rel_b[:, :, :], attw_b[:, 1, :].unsqueeze(1).to_broadcast([P, 2, D]), ALU.mult))
            step(dve.tensor_reduce(relw[:, :], wide[:, :, :], AX.X, ALU.add))
            step(dve.tensor_scalar(relw[:, :], relw[:, :], attb_b[:, 0:1], None, ALU.add))
            at["att"] = n[0]

            dve.memset(acc0[:, :, :], 0.0).then_inc(added0, 1)
            for s in range(2):
                dve.memset(aggr[s][:, :, D:W], 1.0)
            dve.memset(x1[:, :, D:W], 1.0)
            dve.memset(acc1[:, :, :], 0.0).then_inc(added1, 1)

            def hot_matrix(s, key, k=0):
                shape = [P, TG - k, P]
                return dve.tensor_tensor(hot[s][:, k:TG, :], iota_lo[:, :].unsqueeze(1).to_broadcast(shape),
                                         key.unsqueeze(2).to_broadcast(shape), ALU.is_equal)

            def edges0(g, r, n_slot, first):
                s = r % 2
                dve.wait_ge(srec0_in[r], 16 * n_slot)
                if not first:
                    dve.wait_ge(sums0, g - 1)
                hot_matrix(s, srec0[r][:, HOT_POOL:TG, KEY], HOT_POOL).then_inc(hot0_ready, 1)

            def add0(g, s):
                h0 = dve.value_load(tile_hi[0:1, bass.ds(g * TG, 1)], min_val=0, max_val=HI - 1)
                dve.wait_ge(sums0, g + 1)
                for j in range(2):
                    dve.wait_ge(added0, 2 * g + j + 1)
                    view = merged(acc0[:, :, :])[:, j * HALF:][:, bass.ds(h0 * (2 * D), HALF)]
                    dve.tensor_tensor(view, banks[:, 2048 * s + j * HALF:2048 * s + (j + 1) * HALF], view, ALU.add).then_inc(added0, 1)

            dve.wait_ge(table_in, 32)
            for r in range(AHEAD):
                if r >= 2:
                    add0(r - 2, r % 2)
                edges0(r, r, 1, r < 2)
            with dve.Fori(1, SG // AHEAD) as i:
                for r in range(AHEAD):
                    add0(AHEAD * i + r - 2, r % 2)
                    edges0(AHEAD * i + r, r, i + 1, False)
            for s in range(2):
                add0(SG - 2 + s, s)

            def centre(nstep, rows, target, b):
                nstep(dve.tensor_reduce(mean[:, :], rows, AX.X, ALU.add))
                nstep(dve.tensor_scalar(mean[:, :], mean[:, :], 1.0 / D, None, ALU.mult))
                nstep(dve.tensor_tensor(target, rows, mean[:, :].unsqueeze(2).to_broadcast([P, C7, D]), ALU.subtract))
                nstep(dve.tensor_tensor(tmp[:, :, :], target, target, ALU.mult))
                nstep(dve.tensor_reduce(var[b][:, :], tmp[:, :, :], AX.X, ALU.add))
                nstep(dve.tensor_scalar(var[b][:, :], var[b][:, :], 1.0 / D, EPS, ALU.mult, ALU.add))

            def scale(target, b):
                return dve.tensor_tensor(target, target, rstd[b][:, :].unsqueeze(2).to_broadcast([P, C7, D]), ALU.mult)

            step, n = chain(n_step)
            chunks = [slice(c * C7, (c + 1) * C7) for c in range(NC)]
            for c in range(NC + 2):
                if c < NC:
                    rows = th[c % 2][:, :, :]
                    dve.wait_ge(n_th, c + 1)
                    step(dve.tensor_tensor(rows, rows, xs[:, chunks[c], :], ALU.add))
                    centre(step, rows, x1[:, chunks[c], 0:D], c % 2)
                    at["var", c] = n[0]
                if 1 <= c <= NC:
                    dve.wait_ge(n_rstd, c)
                    scale(x1[:, chunks[c - 1], 0:D], (c - 1) % 2).then_inc(n_x1, 1)
                if c >= 2:
                    dve.wait_ge(n_p, c - 1)
                    dve.tensor_copy(q_out[:, chunks[c - 2], :], pair(4).rearrange("p (h w) -> p h w", w=2 * D)[:, :, D:2 * D]).then_inc(n_q, 1)

            def indices1(s, n_slot):
                dve.wait_ge(srec1_in[s], 16 * n_slot)
                dve.tensor_copy(gidx[s][:, :], srec1[s][:, :, DST - D]).then_inc(idx1_ready, 1)

            def sources1(g, s, n_slot, first):
                dve.wait_ge(srec1_in[s], 16 * n_slot)
                if not first:
                    dve.wait_ge(sums1, g - 1)
                hot_matrix(s, srec1[s][:, :, KEY - D]).then_inc(hot1_ready, 1)

            def add_q(g, s, n_slot, first, last=False):
                for q in range(4):
                    if q % 2 == 0:
                        dve.wait_ge(rows1_in[s][q // 2], 16 * TG // 2 * n_slot)
                    if q == 2 and not last:
                        indices1(s, n_slot + 1)
                    dve.wait_ge(pre_done, 4 * g + q + 1)
                    if not first:
                        dve.wait_ge(h_ready, 4 * g + q - 7)
                    dve.tensor_tensor(pre[s][:, 4 * q:4 * q + 4, :],
                                      psum[:, 6 + q % 2, 0:4 * D].rearrange("p (t d) -> p t d", d=D),
                                      qrow[s][:, 4 * q:4 * q + 4, :], ALU.add).then_inc(pre_added, 1)

            def add1(g):
                h0 = dve.value_load(tile_hi[0:1, bass.ds(g * TG, 1)], min_val=0, max_val=HI - 1)
                dve.wait_ge(sums1, g + 1)
                dve.wait_ge(added1, g + 1)
                view = merged(acc1[:, :, :])[:, bass.ds(h0 * W, 3 * L1B * W)].rearrange("p (b n) -> p b n", b=3)
                dve.tensor_tensor(view, psum[:, 0:3, 0:L1B * W], view, ALU.add).then_inc(added1, 1)

            for s in range(2):
                indices1(s, 1)
            for s in range(2):
                sources1(s, s, 1, True)

            def group1(g, s, n_slot, first=False, last=False):
                add_q(g, s, n_slot, first, last)
                add1(g)
                if not last:
                    sources1(g + 2, s, n_slot + 1, False)

            for s in range(2):
                group1(s, s, 1, first=True)
            with dve.Fori(1, SG // 2 - 1) as i:
                for s in range(2):
                    group1(2 * i + s, s, i + 1)
            group1(SG - 2, 0, SG // 2, last=True)
            full = last_group_flag(dve)
            with dve.If(full == 0):
                dve.wait_ge(sums1, SG - 1)
            with dve.Else():
                group1(SG - 1, 1, SG // 2, last=True)

            def add_nodes(c):
                dve.wait_ge(f_hid, c + 1)
                if c >= 2:
                    dve.wait_ge(f_out, c - 1)
                dve.tensor_tensor(hidT[c % 2][0:D, :].rearrange("p (b n) -> p b n", b=2), psum[0:D, 4:6, 0:CW // 2],
                                  x1T[0:D, c * CW:(c + 1) * CW].rearrange("p (b n) -> p b n", b=2), ALU.add).then_inc(f_sum, 1)

            step, n = chain(f_step)
            add_nodes(0)
            for c in range(NC + 1):
                if c + 1 < NC:
                    add_nodes(c + 1)
                if c < NC:
                    rows = th[0][:, :, :]
                    dve.wait_ge(f_out, c + 1)
                    step(dve.tensor_tensor(rows, psum[:, 6 + c % 2, 0:C7 * D].rearrange("p (h d) -> p h d", d=D), x1[:, chunks[c], 0:D], ALU.add))
                    at["out", c] = n[0]
                    centre(step, rows, xs[:, chunks[c], :], c % 2)
                    at["var1", c] = n[0]
                if c >= 1:
                    dve.wait_ge(f_rstd, c)
                    scale(xs[:, chunks[c - 1], :], (c - 1) % 2).then_inc(f_ready, 1)

        @block.sync
        def _(sp):
            sp.wait_ge(memset_done, 4)

            def load_indices(a, t, done):
                full = a[0:(EG - 1) * GE].rearrange("(g p k) -> p g k", p=P, k=TG)
                sp.dma_start(t[:, 0:EG - 1, :], full).then_inc(done, 16)
                sp.dma_start(t[0:TAIL, EG - 1, :], a[(EG - 1) * GE:E].rearrange("(p k) -> p k", k=TG)).then_inc(done, 16)

            load_indices(src, src_i, src_loaded)
            sp.dma_start(by_tile[:, FULL:SS, :], zero_rec[:, :, :].to_broadcast([P, SS - FULL, R])).then_inc(tail_zeroed, 16)
            load_indices(dst, dst_i, loaded)
            load_indices(etype, typ_i, loaded)

            attr_v = attr.rearrange("e a -> (e a)")

            def load_attr(g, s):
                sp.dma_start(merged(attr_in[s][:, :, :]),
                             attr_v[bass.ts(g, GE * A)].rearrange("(p n) -> p n", p=P)).then_inc(attr_loaded[s], 16)

            def load_window(g, s):
                first = sp.value_load(win_i[0:1, bass.ds(g, 1)], min_val=0, max_val=N - WIN)
                sp.dma_start(xwin[s][:, :, :], x[bass.ds(first, WIN), :].rearrange("(w p) d -> p w d", p=P)).then_inc(xwin_in[s], 16)

            for s in range(2):
                load_attr(s, s)
            sp.wait_ge(prep, at["windows"])
            for s in range(2):
                load_window(s, s)
            zero_last_tiles(sp, 0, 3, zeroed)

            def loads(fast):
                with sp.Fori(1, EG // 2) as i:
                    for s in range(2):
                        sp.wait_ge(rec_ready, 2 * i + s - 1)
                        load_attr(2 * i + s, s)
                        if fast:
                            sp.wait_ge(split_step, (2 * i + s - 1) * SPLIT_STEPS)
                            load_window(2 * i + s, s)
                sp.wait_ge(rec_ready, EG - 2)
                sp.dma_start(merged(attr_in[0][0:TAIL, :, :]),
                             attr_v[(EG - 1) * GE * A:E * A].rearrange("(p n) -> p n", p=TAIL)).then_inc(attr_loaded[0], 16)
                if fast:
                    sp.wait_ge(split_step, (EG - 2) * SPLIT_STEPS)
                    load_window(EG - 1, 0)

            sp.wait_ge(prep, at["slow"])
            slow = sp.value_load(slow_i[0:1, 0:1], min_val=0, max_val=P)
            with sp.If(slow == 0):
                loads(True)
            with sp.Else():
                loads(False)

            sp.wait_ge(memset_done, 15)
            last = (HI - 1) * P
            sp.dma_start(xs[:, 0:HI - 1, :], x[0:last, :].rearrange("(h p) d -> p h d", p=P)).then_inc(node_in, 16)
            sp.dma_start(xs[0:N - last, HI - 1, :], x[last:N, :]).then_inc(node_in, 16)
            sp.dma_start(attw_b[:, :, :], att_w.rearrange("(h d) o -> o h d", h=2).to_broadcast([P, 2, D])).then_inc(node_in, 16)
            sp.dma_start(attb_b[:, :], att_b.unsqueeze(0).to_broadcast([P, 1])).then_inc(node_in, 16)
            sp.dma_start(rel_b[:, :, :], rel.unsqueeze(0).to_broadcast([P, 2, D])).then_inc(node_in, 16)
            for w, b, t in ((WT, W_b, W65[:, :]), (ew1[0:D, :], eb1, Eab[:, 0:D]), (ew2, eb2, ew2_65[:, :]),
                            (nw1[0:D, :], nb1, na65[:, :]), (nw2, nb2, nw2_65[:, :])):
                sp.dma_start(t[0:D, :], w).then_inc(node_in, 16)
                sp.dma_start(t[D:W, :], b.unsqueeze(0)).then_inc(node_in, 16)
            sp.dma_start(Eab[0:D, D:2 * D], ew1[D:2 * D, :]).then_inc(node_in, 16)
            sp.dma_start(nb64[:, :], nw1[D:2 * D, :]).then_inc(node_in, 16)
            for q in range(4):
                sp.dma_start(ec_blk[A * q:A * (q + 1), q, :], ew1[2 * D:2 * D + A, :]).then_inc(node_in, 16)

            sp.wait_ge(prep, at["table"])
            for r in range(2):
                sp.dma_start(tile_dram[r:r + 1, :].rearrange("o (p k) -> (o p) k", k=TT), t_out[:, r, :]).then_inc(table_out, 16)
            sp.wait_ge(table_out, 32)
            for r, t in enumerate((tile_hi, tile_slot)):
                sp.dma_start(t[:, :], tile_dram[r:r + 1, :]).then_inc(table_in, 16)

            sp.wait_ge(scattered[0], 16 * TG * (EG // 2 + 1))
            sp.wait_ge(scattered[1], 16 * TG * (EG // 2))

            def load_sorted0(g, r):
                sp.dma_start(merged(srec0[r]), by_lane[:, bass.ts(g, TG * R)]).then_inc(srec0_in[r], 16)

            def load_sorted1(g, s):
                sp.dma_start(srec1[s], by_tile[:, bass.ts(g, TG), D:R]).then_inc(srec1_in[s], 16)

            def used0(count):
                sp.wait_ge(both0_ready, count)
                sp.wait_ge(hot0_ready, count)
                sp.wait_ge(x0_copied, count)

            for r in range(AHEAD):
                load_sorted0(r, r)
            with sp.Fori(1, SG // AHEAD) as i:
                for r in range(AHEAD):
                    used0(AHEAD * i + r - AHEAD + 1)
                    load_sorted0(AHEAD * i + r, r)

            for s in range(2):
                used0(SG - AHEAD + s + 1)
                load_sorted1(s, s)

            for c in range(NC):
                sp.wait_ge(n_q, c + 1)
                sp.dma_start(q_table.rearrange("(h p) d -> p h d", p=P)[:, c * C7:(c + 1) * C7, :],
                             q_out[:, c * C7:(c + 1) * C7, :]).then_inc(q_stored, 16)

            with sp.Fori(1, SG // 2) as i:
                for s in range(2):
                    sp.wait_ge(hot1_ready, 2 * i + s - 1)
                    sp.wait_ge(attr_packed, 2 * i + s - 1)
                    load_sorted1(2 * i + s, s)

            for c in range(NC):
                sp.wait_ge(f_ready, c + 1)
                rows = min(C7 * P, N - c * C7 * P)
                full = rows // P
                o = out[c * C7 * P:c * C7 * P + full * P, :].rearrange("(h p) d -> p h d", p=P)
                sp.dma_start(o, xs[:, c * C7:c * C7 + full, :]).then_inc(stored, 16)
                if rows % P:
                    sp.dma_start(out[N - rows % P:N, :], xs[0:rows % P, HI - 1, :]).then_inc(stored, 16)
            sp.wait_ge(stored, 16 * (NC + 1))

        @block.gpsimd
        def _(pool):
            pool.memset(src_i[:, EG - 1, :], HI * P).then_inc(memset_done, 1)
            pool.memset(dst_i[:, EG - 1, :], N - 1).then_inc(memset_done, 1)
            pool.memset(typ_i[:, EG - 1, :], 0).then_inc(memset_done, 1)
            pool.memset(zero_rec[:, :, :], 0.0).then_inc(memset_done, 1)
            pool.iota(iota_b[:, :], [[1, NB]], base=0, channel_multiplier=0,
                      allow_small_or_imprecise_dtypes=True).then_inc(memset_done, 1)
            pool.memset(ones[:, :], 1.0).then_inc(memset_done, 1)
            pool.iota(iota_lo[:, :], [[1, P]], base=1, channel_multiplier=0,
                      allow_small_or_imprecise_dtypes=True).then_inc(memset_done, 1)
            pool.iota(iota_w[:, :], [[P, 2]], base=0, channel_multiplier=1,
                      allow_small_or_imprecise_dtypes=True).then_inc(memset_done, 1)
            pool.memset(reset[:, :, :], 1.0).then_inc(memset_done, 1)
            pool.memset(first_row[:, :], 0.0).then_inc(memset_done, 1)
            pool.memset(zeros[:, :], 0.0).then_inc(memset_done, 1)
            pool.memset(ec_blk[:, :, :], 0.0).then_inc(memset_done, 1)
            pool.memset(power[:, :], -0.5).then_inc(memset_done, 1)
            pool.memset(Eab[:, :], 0.0).then_inc(memset_done, 1)
            pool.memset(xs[:, HI - 1, :], 0.0).then_inc(memset_done, 1)
            pool.wait_ge(memset_done, 15)
            pool.memset(reset[:, :, 0:1], 0.0).then_inc(memset_done, 1)
            pool.memset(first_row[0:1, :], 1.0).then_inc(memset_done, 1)
            pool.affine_select(out=lower[:, :], in_=ones[:, :], compare_op=ALU.is_gt, fill=0.0, base=0,
                               pattern=[[1, P]], channel_multiplier=-1).then_inc(memset_done, 1)
            pool.affine_select(out=ident[:, :], in_=ones[:, :], compare_op=ALU.is_equal, fill=0.0, base=0,
                               pattern=[[1, P]], channel_multiplier=-1).then_inc(memset_done, 1)
            pool.affine_select(out=ident_h[:, :], in_=ones[:, :], compare_op=ALU.is_equal, fill=0.0, base=0,
                               pattern=[[1, P]], channel_multiplier=-1).then_inc(memset_done, 1)
            pool.iota(t_i[:, 0, :], [[1, TT]], base=0, channel_multiplier=TT).then_inc(memset_done, 1)

            group = pool.alloc_register("group")
            used = pool.alloc_register("used")
            landed = pool.alloc_register("landed")

            def gather(table, rows, index, done):
                for k in range(TG):
                    pool.indirect_dma_start(
                        out=rows[:, k, 0:D], out_offset=None, in_=table,
                        in_offset=bass.IndirectOffsetOnAxis(ap=index[:, k:k + 1], axis=0)).then_inc(done[k * len(done) // TG], 16)

            def scatter(s):
                for k in range(TG):
                    pool.indirect_dma_start(
                        out=sorted_rec, out_offset=bass.IndirectOffsetOnAxis(ap=place[s][:, k:k + 1], axis=0),
                        in_=rec[s][:, k, :], in_offset=None).then_inc(scattered[s], 16)

            def scatters(fast):
                pool.reg_mov(group, 0)
                pool.reg_mov(used, 0)
                pool.reg_mov(landed, 0)

                def one(s, first=False):
                    pool.reg_add(group, group, 1)
                    if not fast:
                        pool.wait_ge(zeroed, 16)
                        pool.wait_ge(xidx_ready, group)
                        if not first:
                            pool.wait_ge(scattered[s], used)
                        gather(x, rec[s], gidx[s], [x_gathered[s]])
                        pool.wait_ge(zeroed, 16)
                        pool.wait_ge(x_gathered[s], landed)
                    pool.wait_ge(zeroed, 16)
                    pool.wait_ge(rec_ready, group)
                    pool.wait_ge(place_ready, group)
                    scatter(s)

                if not fast:
                    pool.reg_add(landed, landed, 16 * TG)
                for s in range(2):
                    one(s, True)
                with pool.Fori(1, EG // 2) as i:
                    if not fast:
                        pool.reg_add(landed, landed, 16 * TG)
                        pool.reg_add(used, used, 16 * TG)
                    for s in range(2):
                        one(s)
                if not fast:
                    pool.reg_add(landed, landed, 16 * TG)
                    pool.reg_add(used, used, 16 * TG)
                one(0)

            zero_last_tiles(pool, 5, NC, zeroed_pool)
            pool.wait_ge(zeroed, 16 * 5 * C7)
            pool.wait_ge(zeroed_pool, 16 * (HI - 5 * C7))
            pool.wait_ge(prep, at["slow"])
            slow = pool.value_load(slow_i[0:1, 0:1], min_val=0, max_val=P)
            with pool.If(slow == 0):
                scatters(True)
            with pool.Else():
                scatters(False)

            def types0(g, r, n_slot, first):
                s = r % 2
                pool.wait_ge(srec0_in[r], 16 * n_slot)
                if not first:
                    pool.wait_ge(sums0, g - 1)
                pool.tensor_tensor(both[s][:, :, D:2 * D], srec0[r][:, :, 0:D],
                                   srec0[r][:, :, TYP].unsqueeze(2).to_broadcast([P, TG, D]), ALU.mult)
                for k in range(HOT_POOL):
                    ins = pool.tensor_scalar(hot[s][:, k, :], iota_lo[:, :], srec0[r][:, k, KEY:KEY + 1], None, ALU.is_equal)
                ins.then_inc(both0_ready, 1)

            for r in range(AHEAD):
                types0(r, r, 1, r < 2)
            with pool.Fori(1, SG // AHEAD) as i:
                for r in range(AHEAD):
                    types0(AHEAD * i + r, r, i + 1, False)

            def roots(c, ready, count, used, done):
                pool.wait_ge(ready, count)
                if c >= 2:
                    pool.wait_ge(used, c - 1)
                pool.tensor_tensor(rstd[c % 2][:, :], var[c % 2][:, :], power[:, :], ALU.pow).then_inc(done, 1)

            pool.wait_ge(att_ready, 1)
            pool.tensor_tensor(att[:, 1, :], att[:, 1, :], att[:, 0, :], ALU.subtract).then_inc(att_ready, 1)
            pool.wait_ge(att_ready, 2)
            pool.wait_ge(added0, 2 * SG + 1)
            for c in range(NC + 3):
                if c < NC:
                    hs = slice(c * C7, (c + 1) * C7)
                    for r in range(2):
                        if c >= 1:
                            pool.wait_ge(n_agg, c)
                        pool.tensor_tensor(part[r][:, :, :], acc0[:, hs, r * D:(r + 1) * D],
                                           att[:, r, hs].unsqueeze(2).to_broadcast([P, C7, D]), ALU.mult).then_inc(agg_step, 1)
                    pool.wait_ge(agg_step, 2 * c + 2)
                    if c >= 2:
                        pool.wait_ge(n_T1, c - 1)
                    pool.tensor_tensor(aggr[c % 2][:, :, 0:D], part[0][:, :, :], part[1][:, :, :], ALU.add).then_inc(n_agg, 1)
                if c >= 3:
                    roots(c - 3, n_step, at["var", c - 3], n_x1, n_rstd)

            pool.wait_ge(q_stored, 16 * NC)
            pool.wait_ge(sums0, SG)
            for s in range(2):
                pool.wait_ge(idx1_ready, s + 1)
                gather(q_table, qrow[s], gidx[s], rows1_in[s])
            pool.reg_mov(group, 2)
            pool.reg_mov(used, 0)

            def next_rows(s):
                pool.reg_add(group, group, 1)
                pool.reg_add(used, used, 4)
                pool.wait_ge(q_stored, 16 * NC)
                pool.wait_ge(idx1_ready, group)
                pool.wait_ge(pre_added, used)
                gather(q_table, qrow[s], gidx[s], rows1_in[s])

            with pool.Fori(1, SG // 2 - 1) as i:
                for s in range(2):
                    next_rows(s)
            next_rows(0)
            full = last_group_flag(pool)
            with pool.If(full == 0):
                pool.wait_ge(pre_added, 4 * (SG - 1))
            with pool.Else():
                next_rows(1)
                pool.wait_ge(pre_added, 4 * SG)
            for c in range(NC):
                roots(c, f_step, at["var1", c], f_ready, f_rstd)

        @block.scalar
        def _(act):
            act.wait_ge(prep, at["hi"])
            for k, b in enumerate(range(B2, NB)):
                if k:
                    act.wait_ge(act_counted, k)
                act.activation(junk_act[:, :], hi_f[:, :], ACT.Sign, bias=half_b[:, b:b + 1],
                               accum_out=signs[:, b:b + 1]).then_inc(act_counted, 1)

            zero_last_tiles(act, 3, 5, zeroed)

            def make_rec(g, s, n_slot, fast):
                act.wait_ge(attr_loaded[s], 16 * (1 if n_slot is None else n_slot + 1))
                if n_slot is not None:
                    act.wait_ge(scattered[s], 16 * TG * n_slot)
                act.activation(rec[s][:, :, D:D + A], attr_in[s][:, :, :], ACT.Copy)
                ins = act.activation(rec[s][:, :, D + A:R], meta[:, bass.ts(g, TG), :], ACT.Copy)
                if fast:
                    act.wait_ge(x_rows_done, g + 1)
                    ins = act.activation(rec[s][:, :, 0:D], banks[:, 2048 + 1024 * s:3072 + 1024 * s].rearrange("p (t d) -> p t d", d=D), ACT.Copy)
                ins.then_inc(rec_ready, 1)

            def records(fast):
                make_rec(0, 0, None, fast)
                make_rec(1, 1, None, fast)
                with act.Fori(1, EG // 2) as i:
                    for s in range(2):
                        make_rec(2 * i + s, s, i, fast)
                make_rec(EG - 1, 0, EG // 2, fast)

            act.wait_ge(prep, max(at["slow"], at["meta"]))
            slow = act.value_load(slow_i[0:1, 0:1], min_val=0, max_val=P)
            with act.If(slow == 0):
                records(True)
            with act.Else():
                records(False)

            act.wait_ge(att_step, at["att"])
            for r in range(2):
                ins = act.activation(att[:, r, :], xw[:, :], ACT.Sigmoid, bias=relw[:, r:r + 1])
            ins.then_inc(att_ready, 1)

            def rows0(g, r, n_slot, first):
                s = r % 2
                act.wait_ge(srec0_in[r], 16 * n_slot)
                if not first:
                    act.wait_ge(sums0, g - 1)
                act.activation(both[s][:, :, 0:D], srec0[r][:, :, 0:D], ACT.Copy).then_inc(x0_copied, 1)
                for j in range(2):
                    if not first:
                        act.wait_ge(added0, 2 * g - 2 + j)
                    act.activation(psum[:, 4 * s + 2 * j:4 * s + 2 * j + 2, :], zeros[:, :].unsqueeze(1).to_broadcast([P, 2, 512]),
                                   ACT.Copy).then_inc(cleared0, 1)

            for r in range(AHEAD):
                rows0(r, r, 1, r < 2)
            with act.Fori(1, SG // AHEAD) as i:
                for r in range(AHEAD):
                    rows0(AHEAD * i + r, r, i + 1, False)

            for c in range(NC + 3):
                if c < NC:
                    act.wait_ge(n_T1, c + 1)
                    if c >= 2:
                        act.wait_ge(n_lin, c - 1)
                    act.activation(nT[c % 2], pair(0)[0:W], ACT.Copy).then_inc(n_T1c, 1)
                if 0 <= c - 1 < NC:
                    k = c - 1
                    act.wait_ge(n_lin, k + 1)
                    if k >= 2:
                        act.wait_ge(n_step, at["var", k - 2])
                    act.activation(th[k % 2][:, :, :], psum[:, 6 + k % 2, 0:C7 * D].rearrange("p (h d) -> p h d", d=D), ACT.Tanh).then_inc(n_th, 1)
                if 0 <= c - 2 < NC:
                    k = c - 2
                    act.wait_ge(n_T2, k + 1)
                    act.activation(x1T[:, k * CW:(k + 1) * CW], pair(2)[0:W], ACT.Copy).then_inc(n_T2c, 1)
                if 0 <= c - 3 < NC:
                    k = c - 3
                    act.wait_ge(n_pq, k + 1)
                    act.activation(ptab[:, k * C7:(k + 1) * C7, :], pair(4).rearrange("p (h w) -> p h w", w=2 * D)[:, :, 0:D], ACT.Copy).then_inc(n_p, 1)

            act.wait_ge(w_step, 1)
            act.activation(ew2T[:, :], psum[0:D, 4, 0:W], ACT.Copy).then_inc(w_copied, 1)
            act.wait_ge(w_step, 2)
            act.activation(M65[:, :], psum[0:W, 5, 0:D], ACT.Copy).then_inc(w_copied, 1)
            for c in range(NC):
                act.wait_ge(x_lin, c + 1)
                act.activation(x1T[0:D, c * CW:(c + 1) * CW].rearrange("p (b n) -> p b n", b=2),
                               psum[0:D, 2 * (c % 2):2 * (c % 2) + 2, 0:CW // 2], ACT.Copy).then_inc(x_linc, 1)

            act.wait_ge(q_stored, 16 * NC)
            for s in range(2):
                act.activation(hrow[s][:, :, D:W], ones[:, 0:TG].unsqueeze(2), ACT.Copy).then_inc(ones_set, 1)

            def edge_group(g, s, n_slot, first):
                act.wait_ge(srec1_in[s], 16 * n_slot)
                if not first:
                    act.wait_ge(attrT_done, g - 1)
                act.activation(attr_in[s][:, :, :], srec1[s][:, :, 0:A], ACT.Copy).then_inc(attr_packed, 1)
                act.wait_ge(attrT_done, g + 1)
                if not first:
                    act.wait_ge(pre_done, 4 * (g - 1))
                act.activation(attrT[s], psum[:, 5, :].rearrange("p (q e) -> p q e", e=P), ACT.Copy).then_inc(attrT_copied, 1)
                for q in range(4):
                    act.wait_ge(hotT_done, 4 * g + q + 1)
                    if not (first and s == 0):
                        act.wait_ge(pre_done, 4 * g + q - 3)
                    act.activation(hotT[:, 4 * q:4 * q + 4, :], psum[:, 3 + q % 2, :].rearrange("p (t e) -> p t e", e=P), ACT.Copy).then_inc(hotT_copied, 1)
                for q in range(4):
                    act.wait_ge(pre_added, 4 * g + q + 1)
                    if not first and q == 0:
                        act.wait_ge(sums1, g - 1)
                    act.activation(hrow[s][:, 4 * q:4 * q + 4, 0:D], pre[s][:, 4 * q:4 * q + 4, :], ACT.Relu).then_inc(h_ready, 1)

            for s in range(2):
                edge_group(s, s, 1, True)
            with act.Fori(1, SG // 2 - 1) as i:
                for s in range(2):
                    edge_group(2 * i + s, s, i + 1, False)
            edge_group(SG - 2, 0, SG // 2, False)
            full = last_group_flag(act)
            with act.If(full == 0):
                act.wait_ge(sums1, SG - 1)
            with act.Else():
                edge_group(SG - 1, 1, SG // 2, False)
                act.wait_ge(sums1, SG)

            for s in range(2):
                act.activation(hidT[s][D:W, :], x1T[D:W, 0:CW], ACT.Copy).then_inc(ones_set, 1)
            for c in range(NC + 1):
                if c < NC:
                    act.wait_ge(f_T, c + 1)
                    if c >= 2:
                        act.wait_ge(f_hid, c - 1)
                    act.activation(nT[c % 2], pair(0)[0:W], ACT.Copy).then_inc(f_Tc, 1)
                if c >= 1:
                    k = c - 1
                    act.wait_ge(f_sum, k + 1)
                    act.activation(hidT[k % 2][0:D, :], hidT[k % 2][0:D, :], ACT.Relu).then_inc(f_hidc, 1)

        @block.tensor
        def _(pe):
            pe.wait_ge(memset_done, MEMSETS)
            pe.wait_ge(prep, at["count"])
            pe.matmul(psum[:, 0, 0:NB], lower[:, :], count[:, :], start=True, stop=True)
            pe.matmul(psum[:, 0, 64:64 + NB], ones[:, :], count[:, :], start=True, stop=True).then_inc(sums_ready, 1)
            pe.wait_ge(prep, at["dst"])
            pe.matmul(psum[:, 1, 0:EG], first_row[:, :],
                      meta[:, :, 1].rearrange("p (g k) -> p g k", k=TG)[:, :, 0], start=True, stop=True).then_inc(sums_ready, 1)
            pe.wait_ge(prep, at["outside"])
            pe.matmul(psum[:, 2, 0:1], ones[:, :], outside[:, :], start=True, stop=True).then_inc(sums_ready, 1)

            def dst_rows(g, s, first=False):
                if not first:
                    pe.wait_ge(win_hot_ready, g - 1)
                for k in range(TG):
                    ins = pe.transpose(win_T[s][:, k * P:(k + 1) * P],
                                       in_win[:, bass.ds(g * TG + k, 1)].to_broadcast([P, P]), ident_h[:, :])
                ins.then_inc(dstT_done, 1)

            def x_rows(g, s, n_slot):
                pe.wait_ge(win_hot_ready, g + 1)
                pe.wait_ge(split_step, (g + 1) * SPLIT_STEPS)
                if n_slot is not None:
                    pe.wait_ge(rec_ready, g - 1)
                for k in range(TG):
                    for n in range(6):
                        ins = pe.matmul(banks[:, 2048 + 1024 * s + k * D:2048 + 1024 * s + (k + 1) * D],
                                        win_hot[s][:, n // 3, k * P:(k + 1) * P], xpart[s][:, n % 3, n // 3, :],
                                        start=(n == 0), stop=(n == 5))
                ins.then_inc(x_rows_done, 1)

            pe.wait_ge(prep, at["slow"])
            slow = pe.value_load(slow_i[0:1, 0:1], min_val=0, max_val=P)
            with pe.If(slow == 0):
                dst_rows(0, 0, True)
                dst_rows(1, 1, True)
                x_rows(0, 0, None)
                dst_rows(2, 0)
                x_rows(1, 1, None)
                with pe.Fori(1, EG // 2) as i:
                    for s in range(2):
                        dst_rows(2 * i + s + 1, 1 - s)
                        x_rows(2 * i + s, s, i)
                x_rows(EG - 1, 0, EG // 2)
            with pe.Else():
                pe.nop()

            slot_regs = [pe.alloc_register(f"slot{k}") for k in range(TG)]
            hi_regs = [pe.alloc_register(f"hi{k}") for k in range(TG)]

            def load_tiles(regs, table, g, top):
                pe.load(regs, table[0:1, bass.ts(g, TG)])
                return [pe.snap(r, min_val=0, max_val=top) for r in regs]

            def sums_of_group0(g, s):
                slots = load_tiles(slot_regs, tile_slot, g, SLOTS - 1)
                pe.wait_ge(cleared0, 2 * g + 2)
                pe.wait_ge(hot0_ready, g + 1)
                pe.wait_ge(x0_copied, g + 1)
                pe.wait_ge(both0_ready, g + 1)
                for k in range(TG):
                    ins = pe.matmul(banks[:, 2048 * s:2048 * s + 2048][:, bass.ts(slots[k], 2 * D)], hot[s][:, k, :], both[s][:, k, :],
                                    start=False, stop=True, skip_group_check=True)
                ins.then_inc(sums0, 1)

            pe.wait_ge(table_in, 32)
            for s in range(2):
                sums_of_group0(s, s)
            with pe.Fori(1, SG // 2) as i:
                for s in range(2):
                    sums_of_group0(2 * i + s, s)

            pe.wait_ge(node_in, 16 * 21)
            pe.wait_ge(added0, 2 * SG + 1)
            for c in range(NC + 3):
                if c < NC:
                    pe.wait_ge(n_agg, c + 1)
                    if c >= 1:
                        pe.wait_ge(n_T1c, c)
                    for h in range(C7):
                        ins = pe.transpose(banks[0:W, h * P:(h + 1) * P], aggr[c % 2][:, h, :], ident[:, :])
                    ins.then_inc(n_T1, 1)
                if 0 <= c - 3 < NC:
                    k = c - 3
                    pe.wait_ge(n_T2c, k + 1)
                    if k >= 1:
                        pe.wait_ge(n_p, k)
                        pe.wait_ge(n_q, k)
                    for h in range(C7):
                        t = k * C7 + h
                        ins = pe.matmul(pair(4)[:, h * P:(h + 1) * P], x1T[:, t * P:(t + 1) * P], Eab[:, :], start=True, stop=True)
                    ins.then_inc(n_pq, 1)
                if c < NC:
                    pe.wait_ge(n_T1c, c + 1)
                    if c >= 2:
                        pe.wait_ge(n_th, c - 1)
                    for h in range(C7):
                        ins = pe.matmul(psum[:, 6 + c % 2, h * D:(h + 1) * D], nT[c % 2][:, h * P:(h + 1) * P], W65[:, :], start=True, stop=True)
                    ins.then_inc(n_lin, 1)
                if 0 <= c - 2 < NC:
                    k = c - 2
                    pe.wait_ge(n_x1, k + 1)
                    if k >= 1:
                        pe.wait_ge(n_T2c, k)
                    for h in range(C7):
                        ins = pe.transpose(pair(2)[0:W, h * P:(h + 1) * P], x1[:, k * C7 + h, :], ident[:, :])
                    ins.then_inc(n_T2, 1)
            pe.wait_ge(n_q, NC)
            pe.wait_ge(n_p, NC)

            pe.transpose(psum[0:D, 4, 0:W], ew2_65[:, :], ident[0:W, 0:W]).then_inc(w_step, 1)
            pe.wait_ge(w_copied, 1)
            pe.matmul(psum[0:W, 5, 0:D], ew2T[:, :], nb64[:, :], start=True, stop=True).then_inc(w_step, 1)
            for c in range(NC):
                if c >= 2:
                    pe.wait_ge(x_linc, c - 1)
                for b in range(2):
                    ins = pe.matmul(psum[0:D, 2 * (c % 2) + b, 0:CW // 2], na65[:, :],
                                    x1T[:, c * CW + b * CW // 2:c * CW + (b + 1) * CW // 2], start=True, stop=True)
                ins.then_inc(x_lin, 1)
            pe.wait_ge(x_linc, NC)
            pe.wait_ge(w_copied, 2)

            ptab_w = merged(ptab[:, :, :])

            def slot_at(v):
                return v * W + (v // L1B) * (512 - L1B * W)

            def edge_group(g, s, n_slot, first):
                slots = load_tiles(slot_regs, tile_slot, g, SLOTS - 1)
                his = load_tiles(hi_regs, tile_hi, g, HI - 1)
                pe.wait_ge(attr_packed, g + 1)
                if not (first and s == 0):
                    pe.wait_ge(attrT_copied, g)
                packed = merged(attr_in[s][:, :, :])
                for q in range(4):
                    ins = pe.transpose(psum[:, 5, q * P:(q + 1) * P], packed[:, 4 * A * q:4 * A * (q + 1)], ident[:, :])
                ins.then_inc(attrT_done, 1)
                pe.wait_ge(hot1_ready, g + 1)

                def transpose_hot(q):
                    if not (first and s == 0 and q < 2):
                        pe.wait_ge(hotT_copied, 4 * g + q - 1)
                    for k in range(4):
                        ins = pe.transpose(psum[:, 3 + q % 2, k * P:(k + 1) * P], hot[s][:, 4 * q + k, :], ident[:, :])
                    ins.then_inc(hotT_done, 1)

                def values(q):
                    if q == 0:
                        pe.wait_ge(attrT_copied, g + 1)
                    if not (first and s == 0 and q < 2):
                        pe.wait_ge(pre_added, 4 * g + q - 1)
                    bank = psum[:, 6 + q % 2, 0:4 * D]
                    pe.matmul(bank, attrT[s][:, q, :], merged(ec_blk[:, :, :]), start=True, stop=False, skip_group_check=True)
                    pe.wait_ge(hotT_copied, 4 * g + q + 1)
                    for k in range(4):
                        ins = pe.matmul(bank[:, k * D:(k + 1) * D], hotT[:, 4 * q + k, :],
                                        ptab_w[:, bass.ts(his[4 * q + k], D)], start=False, stop=True, skip_group_check=True)
                    ins.then_inc(pre_done, 1)

                transpose_hot(0)
                transpose_hot(1)
                values(0)
                transpose_hot(2)
                values(1)
                transpose_hot(3)
                values(2)
                values(3)
                if not (first and s == 0):
                    pe.wait_ge(added1, g + 1)
                for b in range(3):
                    pe.matmul(psum[:, b, :], zeros[:, 0:P], zeros[:, :], start=True, stop=False, skip_group_check=True)
                for k in range(TG):
                    if k % 4 == 0:
                        pe.wait_ge(h_ready, 4 * g + k // 4 + 1)
                    ins = pe.matmul(banks[:, bass.ds(slot_at(slots[k]), W)], hot[s][:, k, :], hrow[s][:, k, :],
                                    start=False, stop=True, skip_group_check=True)
                ins.then_inc(sums1, 1)

            pe.wait_ge(ones_set, 2)
            for s in range(2):
                edge_group(s, s, 1, True)
            with pe.Fori(1, SG // 2 - 1) as i:
                for s in range(2):
                    edge_group(2 * i + s, s, i + 1, False)
            edge_group(SG - 2, 0, SG // 2, False)
            full = last_group_flag(pe)
            with pe.If(full == 0):
                pe.wait_ge(added1, SG)
            with pe.Else():
                edge_group(SG - 1, 1, SG // 2, False)
                pe.wait_ge(added1, SG + 1)

            pe.wait_ge(ones_set, 4)
            H = CW // 2

            def transpose_sums(c):
                if c >= 1:
                    pe.wait_ge(f_Tc, c)
                for h in range(C7):
                    ins = pe.transpose(banks[0:W, h * P:(h + 1) * P], acc1[:, c * C7 + h, :], ident[:, :])
                ins.then_inc(f_T, 1)

            transpose_sums(0)
            for c in range(NC + 1):
                if c + 1 < NC:
                    transpose_sums(c + 1)
                if c < NC:
                    pe.wait_ge(f_Tc, c + 1)
                    if c >= 1:
                        pe.wait_ge(f_sum, c)
                    for b in range(2):
                        ins = pe.matmul(psum[0:D, 4 + b, 0:H], M65[:, :], nT[c % 2][:, b * H:(b + 1) * H], start=True, stop=True)
                    ins.then_inc(f_hid, 1)
                if c >= 1:
                    k = c - 1
                    pe.wait_ge(f_hidc, k + 1)
                    if k >= 2:
                        pe.wait_ge(f_step, at["out", k - 2])
                    for h in range(C7):
                        ins = pe.matmul(psum[:, 6 + k % 2, h * D:(h + 1) * D], hidT[k % 2][:, h * P:(h + 1) * P], nw2_65[:, :], start=True, stop=True)
                    ins.then_inc(f_out, 1)


MEMSETS = 21


_INS = ["x", "src", "dst", "edge_attr_32", "edge_type_2", "L0_gnn_relation_emb", "L0_gnn_att_w", "L0_gnn_att_b",
        "L0_gnn_W_wT", "L0_gnn_W_b", "L1_gnn_ew1", "L1_gnn_eb1", "L1_gnn_ew2", "L1_gnn_eb2", "L1_gnn_nw1",
        "L1_gnn_nb1", "L1_gnn_nw2", "L1_gnn_nb2"]


def kernel(**inputs):
    import numpy as np
    import concourse.bacc as bacc
    from concourse.bass_utils import run_bass_kernel_spmd

    inputs["L0_gnn_W_wT"] = np.asarray(inputs["L0_gnn_W_w"]).T
    nc = bacc.Bacc("TRN2", target_bir_lowering=False, num_devices=1)
    arrays, args = {}, []
    for name in _INS:
        a = np.ascontiguousarray(inputs[name])
        arrays[f"in_{name}"] = a
        args.append(nc.dram_tensor(f"in_{name}", a.shape, mybir.dt.from_np(a.dtype), kind="ExternalInput").ap())
    out = nc.dram_tensor("out_nodes", (N, D), f32, kind="ExternalOutput").ap()
    bass_gnn_two_layers(nc, *args, out)
    r = run_bass_kernel_spmd(nc, [arrays], core_ids=[0])
    return r.results[0]["out_nodes"]
```
